# Optimizing a Trainium2 kernel written in Bass

```python
import numpy as np
import jax
import jax.numpy as jnp

def _softmax(x, axis=-1):
    return jax.nn.softmax(x, axis=axis)

def _gelu(x):
    return jax.nn.gelu(x, approximate=True)

def _silu(x):
    return jax.nn.silu(x)

def _sigmoid(x):
    return jax.nn.sigmoid(x)

def _layernorm(x, axis=-1, eps=1e-05):
    m = jnp.mean(x, axis=axis, keepdims=True)
    v = jnp.var(x, axis=axis, keepdims=True)
    return (x - m) / jnp.sqrt(v + eps)

def _scatter_add(tgt, idx, src, axis=0):
    return tgt.at[idx].add(src)

def _segment_sum(src, seg, n):
    return jax.ops.segment_sum(src, seg, n)
kernel_name = 'mk_macaron_d1_jaxref_r8_ccbdac'

def setup_inputs(seed: int=0):
    np.random.seed(seed)
    _w = jnp.asarray

    def _L0_attn_setup():
        import jax, jax.numpy as jnp
        import numpy as np
        DIM = 128
        N_HEADS = 16
        HEAD_DIM = DIM // N_HEADS
        FREQS = [31.0, 37.0, 41.0, 43.0, 47.0]
        TWO_PI = 2.0 * float(np.pi)
        key = jax.random.key(seed)
        ks = jax.random.split(key, 16)
        B, L = (2, 128)
        s = 0.02
        inp = {'x': jax.random.normal(ks[0], (B, L, DIM), dtype=jnp.float32), 'Wq': jax.random.normal(ks[1], (DIM, DIM), dtype=jnp.float32) * s, 'bq': jnp.zeros((DIM,), dtype=jnp.float32), 'Wk': jax.random.normal(ks[2], (DIM, DIM), dtype=jnp.float32) * s, 'bk': jnp.zeros((DIM,), dtype=jnp.float32), 'Wv': jax.random.normal(ks[3], (DIM, DIM), dtype=jnp.float32) * s, 'bv': jnp.zeros((DIM,), dtype=jnp.float32), 'Wo': jax.random.normal(ks[4], (DIM, DIM), dtype=jnp.float32) * s, 'bo': jnp.zeros((DIM,), dtype=jnp.float32), 'alpha': jax.random.normal(ks[5], (N_HEADS, len(FREQS)), dtype=jnp.float32) * 0.1, 'phi': jax.random.uniform(ks[6], (N_HEADS, len(FREQS)), dtype=jnp.float32) * TWO_PI, 'temperature': jnp.ones((1,), dtype=jnp.float32), 'gamma': jnp.ones((DIM,), dtype=jnp.float32), 'beta': jnp.zeros((DIM,), dtype=jnp.float32)}
        return inp
    _L0_attn_in = _L0_attn_setup()

    def _L0_ffn_setup():
        import jax, jax.numpy as jnp
        import numpy as np
        D_MODEL = 128
        key = jax.random.key(seed)
        k_x, k_w, k_a1, k_a2 = jax.random.split(key, 4)
        x = jax.random.normal(k_x, (4, 256, D_MODEL), dtype=jnp.float32)
        weight = jax.random.normal(k_w, (D_MODEL, D_MODEL), dtype=jnp.float32) * 0.02
        aux_weight1 = jax.random.normal(k_a1, (D_MODEL, D_MODEL), dtype=jnp.float32) * 0.02
        aux_weight2 = jax.random.normal(k_a2, (D_MODEL, D_MODEL), dtype=jnp.float32) * 0.02
        bias = jnp.zeros((D_MODEL,), dtype=jnp.float32)
        return {'x': x, 'weight': weight, 'aux_weight1': aux_weight1, 'aux_weight2': aux_weight2, 'bias': bias}
    _L0_ffn_in = _L0_ffn_setup()
    _d = {'L0_attn_x': _L0_attn_in['x'], 'L0_attn_Wq': _L0_attn_in['Wq'], 'L0_attn_bq': _L0_attn_in['bq'], 'L0_attn_Wk': _L0_attn_in['Wk'], 'L0_attn_bk': _L0_attn_in['bk'], 'L0_attn_Wv': _L0_attn_in['Wv'], 'L0_attn_bv': _L0_attn_in['bv'], 'L0_attn_Wo': _L0_attn_in['Wo'], 'L0_attn_bo': _L0_attn_in['bo'], 'L0_attn_alpha': _L0_attn_in['alpha'], 'L0_attn_phi': _L0_attn_in['phi'], 'L0_attn_temperature': _L0_attn_in['temperature'], 'L0_attn_gamma': _L0_attn_in['gamma'], 'L0_attn_beta': _L0_attn_in['beta'], 'L0_ffn_weight': _L0_ffn_in['weight'], 'L0_ffn_aux_weight1': _L0_ffn_in['aux_weight1'], 'L0_ffn_aux_weight2': _L0_ffn_in['aux_weight2'], 'L0_ffn_bias': _L0_ffn_in['bias']}
    _x0 = _d['L0_attn_x']
    _d['L0_attn_x'] = jax.random.normal(jax.random.fold_in(jax.random.key(seed), 1), (16, 512, 128), dtype=_x0.dtype)
    del _x0
    return _d

def reference(L0_attn_x, L0_attn_Wq, L0_attn_bq, L0_attn_Wk, L0_attn_bk, L0_attn_Wv, L0_attn_bv, L0_attn_Wo, L0_attn_bo, L0_attn_alpha, L0_attn_phi, L0_attn_temperature, L0_attn_gamma, L0_attn_beta, L0_ffn_weight, L0_ffn_aux_weight1, L0_ffn_aux_weight2, L0_ffn_bias):

    def _L0_attn_ref(x, Wq, bq, Wk, bk, Wv, bv, Wo, bo, alpha, phi, temperature, gamma, beta):
        import jax, jax.numpy as jnp
        import numpy as np
        DIM = 128
        N_HEADS = 16
        HEAD_DIM = DIM // N_HEADS
        FREQS = [31.0, 37.0, 41.0, 43.0, 47.0]
        TWO_PI = 2.0 * float(np.pi)
        B, L, D = x.shape
        H, hd = (N_HEADS, HEAD_DIM)
        q = (x @ Wq.T + bq).reshape(B, L, H, hd).transpose(0, 2, 1, 3)
        k = (x @ Wk.T + bk).reshape(B, L, H, hd).transpose(0, 2, 1, 3)
        v = (x @ Wv.T + bv).reshape(B, L, H, hd).transpose(0, 2, 1, 3)
        sim = jnp.einsum('bhid,bhjd->bhij', q, k) / jnp.sqrt(jnp.asarray(hd, x.dtype))
        temp = jnp.abs(temperature)[0] + 0.1
        sim = sim / temp
        scores = jnp.zeros_like(sim)
        for fi, freq in enumerate(FREQS):
            a = alpha[:, fi][None, :, None, None]
            p = phi[:, fi][None, :, None, None]
            scores = scores + a * jnp.sin(TWO_PI * sim / freq + p)
        w = jax.nn.sigmoid(scores)
        w = w / (jnp.sum(w, axis=-1, keepdims=True) + 1e-10)
        out = jnp.einsum('bhij,bhjd->bhid', w, v)
        out = out.transpose(0, 2, 1, 3).reshape(B, L, D)
        out = out @ Wo.T + bo
        mu = jnp.mean(out, axis=-1, keepdims=True)
        var = jnp.mean(jnp.square(out - mu), axis=-1, keepdims=True)
        return (out - mu) / jnp.sqrt(var + 1e-05) * gamma + beta

    def _L0_ffn_ref(x, weight, aux_weight1, aux_weight2, bias):
        import jax, jax.numpy as jnp
        import numpy as np
        D_MODEL = 128
        h = jnp.einsum('btc,cd->btd', x, weight)
        h = jnp.einsum('btc,cd->btd', h, aux_weight1)
        h = jnp.einsum('btc,cd->btd', h, aux_weight2)
        return jnp.tanh(h + bias)
    x = L0_attn_x
    x = x + 0.5 * _L0_ffn_ref(_layernorm(x, axis=-1), L0_ffn_weight, L0_ffn_aux_weight1, L0_ffn_aux_weight2, L0_ffn_bias)
    x = x + _L0_attn_ref(_layernorm(x, axis=-1), L0_attn_Wq, L0_attn_bq, L0_attn_Wk, L0_attn_bk, L0_attn_Wv, L0_attn_bv, L0_attn_Wo, L0_attn_bo, L0_attn_alpha, L0_attn_phi, L0_attn_temperature, L0_attn_gamma, L0_attn_beta)
    x = x + 0.5 * _L0_ffn_ref(_layernorm(x, axis=-1), L0_ffn_weight, L0_ffn_aux_weight1, L0_ffn_aux_weight2, L0_ffn_bias)
    return x

_drawn_inputs = setup_inputs


def setup_inputs(seed=0):
    import zlib

    import numpy as np

    out = dict(_drawn_inputs(seed))
    spreads = {'L0_attn_bq': (0.0, 2.0),
     'L0_attn_bk': (0.0, 2.0),
     'L0_attn_bv': (0.0, 0.1),
     'L0_attn_bo': (0.0, 0.1),
     'L0_attn_gamma': (1.0, 0.2),
     'L0_attn_beta': (0.0, 0.1),
     'L0_ffn_bias': (0.0, 0.492)}
    factors = {'L0_attn_Wq': 43.312,
     'L0_attn_Wk': 41.056,
     'L0_attn_alpha': 30.368,
     'L0_attn_phi': 35.609,
     'L0_ffn_weight': 7.804,
     'L0_ffn_aux_weight1': 7.791,
     'L0_ffn_aux_weight2': 7.921,
     'L0_attn_Wv': 2.783}
    for name, (base, spread) in spreads.items():
        noise = np.random.default_rng([zlib.crc32(name.encode()), seed]).standard_normal(out[name].shape)
        drawn = base * np.exp(spread * noise) if base else spread * noise
        out[name] = jnp.asarray(drawn.astype(out[name].dtype))
    for name, factor in factors.items():
        out[name] = (out[name] * factor).astype(out[name].dtype)
    return out
```

```python
import numpy as np
import concourse.bass as bass
from concourse import mybir
from contextlib import ExitStack

B, L, D = 16, 512, 128
H, HD = 16, 8
FREQS = (31.0, 37.0, 41.0, 43.0, 47.0)
NF = len(FREQS)
P = 128
TC = L // P
G = 4
NQ = H // G
R = P // G
HALVES = 2
QPH = NQ // HALVES
UNITS = QPH * G
SINS = 5
SETS = 3
SETS_PER_SINE = 2
MAGIC = 1.5 * 2.0 ** 23
TWO_PI_DOWN = float(np.nextafter(np.float32(2 * np.pi), np.float32(0)))
EPS = 1e-5
TINY = 1e-18

C_IDENT, C_HEADS, C_REP, C_PHIREP = 0, 128, 256, 384
C_QG, C_QB, C_KG, C_KB, C_MPOS, C_MNEG, C_MROW, C_QROW, C_ONE = 512, 513, 514, 515, 516, 520, 524, 525, 526
NCONST = 527


def constants():
    c = np.zeros((P, NCONST), np.float32)
    c[:, C_IDENT:C_IDENT + P] = np.eye(P)
    r = np.arange(P) % R
    g = np.arange(P) // R
    for k in range(H):
        c[k, C_HEADS + HD * k:C_HEADS + HD * (k + 1)] = 1.0
    for k in range(P):
        head, d = (k % R) // HD, k % HD
        for part in range(3):
            c[k, C_REP + R * head + HD * part + d] = 1.0
    for k in range(G):
        c[k, C_PHIREP + R * k + 24:C_PHIREP + R * k + 26] = 1.0
    q_low = (r < 8) | (r == 25)
    k_low = (r >= 8) & (r < 16)
    c[:, C_QG], c[:, C_QB] = np.where(q_low, 1, -1), np.where(q_low, 1, 0)
    c[:, C_KG], c[:, C_KB] = np.where(k_low, 1, -1), np.where(k_low, 1, 0)
    for head in range(G):
        c[:, C_MPOS + head] = (g == head) & (r < 28)
        c[:, C_MNEG + head] = -1.0 * ((g == head) & (r < 26))
    c[:, C_MROW] = np.where(r == 26, MAGIC, np.where(r == 27, -MAGIC, 0))
    c[:, C_QROW] = r < 24
    c[:, C_ONE] = (r >= 24) & (r < 28)
    return c


def build(nc, x, Wq, bq, Wk, bk, Wv, bv, Wo, bo, alpha, phi, temperature, gamma, beta,
          W1, W2, W3, bias, consts, out):
    F32, F32R = mybir.dt.float32, mybir.dt.float32r
    ALU, ACT = mybir.AluOpType, mybir.ActivationFunctionType
    ctx = ExitStack()
    with ctx:
        def sb(name, shape, dt=F32):
            return ctx.enter_context(nc.sbuf_tensor(name, shape, dt))

        def sem(name):
            return ctx.enter_context(nc.semaphore(name))

        x1_d = nc.dram_tensor("x1_scratch", (B, P, TC, D), F32).ap()
        hT_d = nc.dram_tensor("hT_scratch", (B, D, L), F32).ap()
        oT_d = nc.dram_tensor("oT_scratch", (B, D, L), F32).ap()
        den_d = nc.dram_tensor("den_scratch", (B, H, L), F32).ap()
        rden_d = nc.dram_tensor("rden_scratch", (B, H, L), F32).ap()

        cst = sb("cst", [P, NCONST])
        ident = cst[:, C_IDENT:C_IDENT + P]
        wnat = sb("wnat", [P, 7, P])
        wq_s = sb("wq_s", [P, NQ, P])
        wk_s = sb("wk_s", [P, NQ, P])
        wvT = sb("wvT", [P, P])
        woT = sb("woT", [P, P])
        w1T = sb("w1T", [P, P])
        w12T = sb("w12T", [P, P])
        wf = sb("wf", [P, P])
        rows = sb("rows", [1, 5, P])
        misc = sb("misc", [1, H * NF + 1])
        bqk = sb("bqk", [R, 2, NQ])
        phi4 = sb("phi4", [G, NQ, NF])
        phit = sb("phit", [G, NQ, NF])
        ones = sb("ones", [P, P])
        alpha_bc = sb("alpha_bc", [P, H * NF + 1])
        a_neg = sb("a_neg", [P, H, NF])
        a_abs = sb("a_abs", [P, H, NF])
        alpha_s = sb("alpha_s", [P, H, NF])
        ratio = sb("ratio", [P, H, NF - 1])
        gb_bc = sb("gb_bc", [P, 2, P])
        bq_c = sb("bq_c", [P, NQ])
        bk_c = sb("bk_c", [P, NQ])
        itemp = sb("itemp", [P, 3])
        s_f = sb("s_f", [P, NF])
        s_tab = sb("s_tab", [P, NQ, NF])
        gs = sb("gs", [P, NQ, NF])
        bs = sb("bs", [P, NQ, NF])
        mhalf = sb("mhalf", [P, TC])

        sins = sb("sins", [P, SINS, TC * L])
        acc = sb("acc", [P, UNITS, TC * L])
        q_r = sb("q_r", [P, QPH, NF, L], F32R)
        k_r = sb("k_r", [P, QPH, 2, G, L], F32R)
        hi_r = sb("hi_r", [P, 2, L], F32R)
        xq = sb("xq", [P, L])
        xk = sb("xk", [P, 2, L])
        ks = sb("ks", [P, L])
        v_s = sb("v_s", [P, NQ, TC, G, R])
        hT = sb("hT", [P, L])
        o_sb = sb("o_sb", [P, L])
        den_a = sins[:, 0, 0:B * H * L // P]

        NS = 4

        def tile(k):
            return [acc[:, k, L * j:L * (j + 1)].rearrange("p (t d) -> p t d", t=TC) for j in range(NS)]

        xin, xn, xnT, th, x1t, hn, hTo, yv = (tile(k) for k in range(UNITS))
        rd16 = [sins[0:H, 1, L * j:L * (j + 1)] for j in range(NS)]
        stats = sb("stats", [P, NS, 3, TC, 6])
        mv = sb("mv", [P, NS, 3, TC, 2])
        vare = sb("vare", [P, NS, 3, TC])
        rstd = sb("rstd", [P, NS, 3, TC])

        ps = ctx.enter_context(nc.psum_tensor("ps", [P, 8, L], F32))
        BK_A, BK_B = 6, 7

        s_const = sem("consts_loaded")
        s_ones = sem("ones_set")
        s_wps = sem("setup_product_ready")
        s_wsb = sem("setup_product_copied")
        s_tab_step = sem("setup_table_step")
        s_setup = sem("setup_done")
        a_x = [sem(f"a_x_loaded_{j}") for j in range(NS)]
        a_step = sem("ac_vector_step")
        a_var = sem("ac_variance_ready")
        a_rstd = sem("ac_rstd_ready")
        a_norm = sem("ac_normalised")
        a_tp = sem("ac_transposed_in_psum")
        a_tcp = sem("ac_transposed_in_sbuf")
        a_ff = sem("ac_ffn_in_psum")
        a_th = sem("ac_tanh_ready")
        a_x1 = sem("a_x1_ready")
        a_stx = sem("a_x1_stored")
        a_sth = sem("a_hT_stored")
        b_h = sem("b_hT_loaded")
        b_kps = sem("b_k_in_psum")
        b_qps = sem("b_q_in_psum")
        b_vps = sem("b_v_in_psum")
        b_xk = sem("b_k_biased")
        b_xq = sem("b_q_biased")
        b_v = sem("b_v_copied")
        b_step = sem("b_vector_split_step")
        b_ks = sem("b_k_split")
        b_kr = sem("b_k_sides_ready")
        b_qr = sem("b_q_sides_ready")
        b_t = sem("b_angles_ready")
        b_sin = sem("b_sines_ready")
        b_fma = sem("b_sine_added")
        b_sig = sem("b_sigmoids_ready")
        b_pv = sem("b_pv_in_psum")
        b_o = sem("b_pv_copied")
        b_st = sem("b_heads_stored")
        c_ld = [sem(f"c_loaded_{j}") for j in range(NS)]
        c_den = sem("c_denominators_moved")
        c_eps = sem("c_denominators_guarded")
        c_rden = sem("c_reciprocals_ready")
        c_sp = sem("c_reciprocals_in_psum")
        c_on = sem("c_heads_normalised")
        c_y = sem("c_projection_in_psum")
        c_y2 = sem("c_attention_added")
        c_out = sem("c_out_ready")
        c_st = sem("c_out_stored")

        N_CONST = 18

        s_passed = {name: sem(f"waits_passed_by_{name}") for name in ("sync", "pool", "vector")}

        def alone(eng, name):
            eng.sem_inc(s_passed[name], 1)

        block = ctx.enter_context(nc.Block())

        SETS_HALF = UNITS * NF * SETS_PER_SINE
        SETS_ROW = HALVES * SETS_HALF
        SINES_HALF = UNITS * NF
        UNITS_ROW = HALVES * UNITS
        SET_CREDIT, SINE_CREDIT, PV_CREDIT, COPY_CREDIT = SETS, SINS, QPH, 1
        STORES = G + 1
        STORE_CREDIT = 16

        def order(half):
            return [(2 * pair + a, f) for pair in range(UNITS // 2) for f in range(NF) for a in range(2)]

        ADDS_HALF = UNITS * (NF - 1)
        ADDS_ROW = HALVES * ADDS_HALF

        def added(m):
            return len([f for _, f in order(0)[:m + 1] if f > 0])

        def last_addition(unit):
            return added(max(m for m, (u, f) in enumerate(order(0)) if u == unit))

        def freed(m):
            return added(m + 2 if order(0)[m][1] == 0 else m)

        @block.sync
        def _(sp):
            sp.dma_start(cst[:, :], consts).then_inc(s_const, 16)
            for n, w in enumerate((Wq, Wk, Wv, Wo, W1, W2, W3)):
                sp.dma_start(wnat[:, n, :], w).then_inc(s_const, 16)
            for n, v in enumerate((bv, bo, bias, gamma, beta)):
                sp.dma_start(rows[0:1, n, :], v.rearrange("(a n) -> a n", a=1)).then_inc(s_const, 16)
            sp.dma_start(misc[0:1, 0:H * NF], alpha.rearrange("(a h) f -> a (h f)", a=1)).then_inc(s_const, 16)
            sp.dma_start(misc[0:1, H * NF:], temperature.rearrange("(a n) -> a n", a=1)).then_inc(s_const, 16)
            sp.dma_start(phi4[:, :, :], phi.rearrange("(q g) f -> g q f", g=G)).then_inc(s_const, 16)

            sp.dma_start(bqk[:, 0, :], bq.rearrange("(q p) -> p q", p=R), allow_slow_non_contiguous=True).then_inc(s_const, 16)
            sp.dma_start(bqk[:, 1, :], bk.rearrange("(q p) -> p q", p=R), allow_slow_non_contiguous=True).then_inc(s_const, 16)

            def load_rows(i):
                for j in range(NS):
                    sp.dma_start(xin[j], x[bass.ds(i * NS + j, 1)].rearrange("o (p t) d -> p (o t) d", t=TC)).then_inc(a_x[j], 16)

            with sp.Fori(0, B // NS) as i:
                load_rows(i)
                for j in range(NS):
                    sp.wait_ge(a_x1, i * NS + j + 1)
                    alone(sp, "sync")
                    sp.dma_start(x1_d[bass.ds(i * NS + j, 1)].rearrange("o p t d -> p (o t) d"), x1t[j]).then_inc(a_stx, 16)
                for j in range(NS):
                    sp.wait_ge(a_tcp, i * 2 * NS + NS + j + 1)
                    alone(sp, "sync")
                    sp.dma_start(hT_d[bass.ds(i * NS + j, 1)].rearrange("o d l -> d (o l)"),
                                 hTo[j].rearrange("p t d -> p (t d)")).then_inc(a_sth, 16)
            sp.wait_ge(a_stx, B * 16)
            sp.wait_ge(a_sth, B * 16)

            sp.sem_inc(b_st, STORE_CREDIT)
            sp.dma_start(hT[:, :], hT_d[0]).then_inc(b_h, 16)

            def store_heads(i, q):
                sp.wait_ge(b_o, i * NQ + q + 1 + COPY_CREDIT)
                alone(sp, "sync")
                for g in range(G):
                    sp.dma_start(oT_d[bass.ds(i, 1), (q * G + g) * HD:(q * G + g + 1) * HD, :].rearrange("o d l -> d (o l)"),
                                 o_sb[R * g:R * g + HD, :]).then_inc(b_st, 16)
                sp.dma_start(den_d[bass.ds(i, 1), q * G:(q + 1) * G, :].rearrange("o h l -> h (o l)"),
                             o_sb[HD:HD + R * (G - 1) + 1:R, :]).then_inc(b_st, 16)

            def row(i, last):
                for half in range(HALVES):
                    if half == 0 and not last:
                        sp.wait_ge(b_vps, i * NQ + NQ)
                        alone(sp, "sync")
                        sp.dma_start(hT[:, :], hT_d[bass.ds(i + 1, 1)].rearrange("o d l -> d (o l)")).then_inc(b_h, 16)
                    for q in range(QPH * half, QPH * (half + 1)):
                        store_heads(i, q)
            with sp.Fori(0, B - 1) as i:
                row(i, False)
            row(B - 1, True)
            sp.wait_ge(b_st, B * NQ * STORES * 16 + STORE_CREDIT)
            sp.dma_start(den_a[:, :], den_d.rearrange("b h (s l) -> (b h s) l", s=1).rearrange("(p r) l -> p (r l)", p=P)).then_inc(c_den, 16)
            sp.wait_ge(c_rden, 1)
            sp.dma_start(rden_d.rearrange("b h l -> (b h) l").rearrange("(p r) l -> p (r l)", p=P), den_a[:, :]).then_inc(c_den, 16)
            sp.wait_ge(c_den, 32)

            with sp.Fori(0, B // NS) as i:
                for j in range(NS):
                    sp.dma_start(xin[j].rearrange("p t d -> p (t d)"),
                                 oT_d[bass.ds(i * NS + j, 1)].rearrange("o d l -> d (o l)")).then_inc(c_ld[j], 16)
                    sp.dma_start(x1t[j], x1_d[bass.ds(i * NS + j, 1)].rearrange("o p t d -> p (o t) d")).then_inc(c_ld[j], 16)
                    sp.dma_start(rd16[j], rden_d[bass.ds(i * NS + j, 1)].rearrange("o h l -> h (o l)")).then_inc(c_ld[j], 16)
                for j in range(NS):
                    sp.wait_ge(c_out, i * NS + j + 1)
                    alone(sp, "sync")
                    sp.dma_start(out[bass.ds(i * NS + j, 1)].rearrange("o (p t) d -> p (o t) d", t=TC), th[j]).then_inc(c_st, 16)
                sp.wait_ge(c_st, (i + 1) * NS * 16)
                alone(sp, "sync")
            sp.wait_ge(c_st, B * 16)

        @block.tensor
        def _(pe):
            pe.wait_ge(s_const, N_CONST * 16)
            pe.wait_ge(s_ones, 1)
            one = ones[0:1, 0:P]
            nc.tensor.transpose(ps[:, 0, 0:P], wnat[:, 2, :], ident)
            nc.tensor.transpose(ps[:, 0, P:2 * P], wnat[:, 3, :], ident)
            nc.tensor.transpose(ps[:, 0, 2 * P:3 * P], wnat[:, 4, :], ident).then_inc(s_wps, 1)
            for q in range(NQ):
                rep = slice(R * q, R * (q + 1))
                for n in range(2):
                    mm = nc.tensor.matmul(ps[:, 1 + q, P * n:P * (n + 1)], wnat[rep, n, :],
                                          cst[rep, C_REP:C_REP + P], start=True, stop=True)
            mm.then_inc(s_wps, 1)
            nc.tensor.matmul(ps[:, 5, 0:H * NF + 1], one, misc[0:1, :], start=True, stop=True)
            nc.tensor.matmul(ps[:, 5, P:P + 2 * P], one, rows[0:1, 3:5, :], start=True, stop=True).then_inc(s_wps, 1)
            nc.tensor.matmul(ps[:, 6, 0:2 * NQ], cst[0:R, C_REP:C_REP + P], bqk[:, :, :], start=True, stop=True)
            pe.wait_ge(s_tab_step, 1)
            nc.tensor.matmul(ps[:, 6, P:P + NQ * NF], cst[0:G, C_PHIREP:C_PHIREP + P], phit[:, :, :],
                             start=True, stop=True).then_inc(s_wps, 1)
            pe.wait_ge(s_wsb, 3)
            nc.tensor.matmul(ps[:, 7, 0:P], wnat[:, 5, :], w1T[:, :], start=True, stop=True).then_inc(s_wps, 1)
            pe.wait_ge(s_wsb, 4)
            nc.tensor.matmul(ps[:, 7, P:2 * P], w12T[:, :], wnat[:, 6, :], start=True, stop=True).then_inc(s_wps, 1)
            pe.wait_ge(s_setup, 1)

            def transposes(src, j, norm_at):
                pe.wait_ge(a_norm, norm_at)
                for t in range(TC):
                    mm = nc.tensor.transpose(ps[:, 2 * j, P * t:P * (t + 1)], src[j][:, t, :], ident)
                mm.then_inc(a_tp, 1)

            def feed_forward(j, copied_at):
                pe.wait_ge(a_tcp, copied_at)
                for t in range(TC):
                    nc.tensor.matmul(ps[:, 2 * j + 1, P * t:P * (t + 1)], xnT[j][:, t, :], wf[:, :], start=True, stop=False)
                    mm = nc.tensor.matmul(ps[:, 2 * j + 1, P * t:P * (t + 1)], one, rows[0:1, 2, :], start=False, stop=True)
                mm.then_inc(a_ff, 1)

            with pe.Fori(0, B // NS) as i:
                for j in range(NS):
                    transposes(xn, j, i * 2 * NS + j + 1)
                for j in range(NS):
                    feed_forward(j, i * 2 * NS + j + 1)
                for j in range(NS):
                    transposes(hn, j, i * 2 * NS + NS + j + 1)
                pe.wait_ge(a_tcp, (i + 1) * 2 * NS)

            def project(b, q, first):
                n = b * NQ + q
                if q % QPH == 0:
                    pe.wait_ge(b_h, (b + 1) * 16)
                    if not first:
                        pe.wait_ge(b_o, n - QPH + COPY_CREDIT)
                        pe.wait_ge(b_xq, n)
                else:
                    pe.wait_ge(b_v, n)
                    pe.wait_ge(b_xq, n)
                nc.tensor.matmul(ps[:, BK_A, :], wk_s[:, q, :], hT[:, :], start=True, stop=True).then_inc(b_kps, 1)
                nc.tensor.matmul(ps[:, BK_B, :], wq_s[:, q, :], hT[:, :], start=True, stop=True).then_inc(b_qps, 1)
                pe.wait_ge(b_xk, n + 1)
                for t in range(TC):
                    o = ps[:, BK_A, P * t:P * t + R]
                    nc.tensor.matmul(o, hT[:, P * t:P * (t + 1)], wvT[:, R * q:R * (q + 1)], start=True, stop=False)
                    mm = nc.tensor.matmul(o, one, rows[0:1, 0, R * q:R * (q + 1)], start=False, stop=True)
                mm.then_inc(b_vps, 1)

            def angles(b, half, lo, hi):
                for s in range(lo, hi):
                    unit, f = order(half)[s // SETS_PER_SINE]
                    slot, g = unit // G, unit % G
                    n = b * SETS_ROW + half * SETS_HALF + s
                    if s < SETS:
                        if s == 0:
                            pe.wait_ge(b_sin, b * SETS_ROW + half * SETS_HALF + SET_CREDIT)
                    else:
                        pe.wait_ge(b_sin, n - SETS + 1 + SET_CREDIT)
                    if s == 0 or s == G * NF * SETS_PER_SINE:
                        pe.wait_ge(b_kr, b * NQ + half * QPH + slot + 1)
                        pe.wait_ge(b_qr, b * NQ + half * QPH + slot + 1)
                    for t in range(SETS_PER_SINE):
                        block_at = (s % SETS_PER_SINE) * SETS_PER_SINE + t
                        keys = slice(P * block_at, P * (block_at + 1))
                        o = ps[:, (s % SETS) * SETS_PER_SINE + t, :]
                        nc.tensor.matmul(o, k_r[:, slot, 0, g, keys], q_r[:, slot, f, :], start=True, stop=False)
                        mm = nc.tensor.matmul(o, k_r[:, slot, 1, g, keys], q_r[:, slot, f, :], start=False, stop=True)
                    mm.then_inc(b_t, 1)

            def attend(b, q):
                n = b * NQ + q
                pe.wait_ge(b_sig, b * UNITS_ROW + G * (q + 1))
                pe.wait_ge(b_o, n + COPY_CREDIT)
                for t in range(TC):
                    for g in range(G):
                        mm = nc.tensor.matmul(ps[R * g:R * (g + 1), BK_A, :], v_s[:, q, t, g, :],
                                              acc[:, (q % QPH) * G + g, L * t:L * (t + 1)],
                                              start=(t == 0), stop=(t == TC - 1))
                mm.then_inc(b_pv, 1)

            def project_half(b, half, first=False):
                for q in range(QPH * half, QPH * (half + 1)):
                    project(b, q, first)
                pe.wait_ge(b_v, b * NQ + QPH * (half + 1))

            pe.sem_inc(b_pv, PV_CREDIT)
            project_half(0, 0, first=True)

            def row(b, last):
                for half in range(HALVES):
                    angles(b, half, 0, SETS_HALF)
                    nb, nh = (b, 1) if half == 0 else (b + 1, 0)
                    if not (half == 1 and last):
                        project_half(nb, nh)
                    for q in range(QPH * half, QPH * (half + 1)):
                        attend(b, q)
            with pe.Fori(0, B - 1) as b:
                row(b, False)
            row(B - 1, True)

            with pe.Fori(0, B // NS) as i:
                for j in range(NS):
                    pe.wait_ge(c_ld[j], (i + 1) * 48)
                    nc.tensor.matmul(ps[:, 2 * j, :], cst[0:H, C_HEADS:C_HEADS + P], rd16[j], start=True, stop=True).then_inc(c_sp, 1)
                for j in range(NS):
                    pe.wait_ge(c_on, i * NS + j + 1)
                    for t in range(TC):
                        o = ps[:, 2 * j + 1, P * t:P * (t + 1)]
                        nc.tensor.matmul(o, xin[j][:, t, :], woT[:, :], start=True, stop=False)
                        mm = nc.tensor.matmul(o, one, rows[0:1, 1, :], start=False, stop=True)
                    mm.then_inc(c_y, 1)
                for j in range(NS):
                    transposes(xn, j, 2 * B + i * NS + j + 1)
                for j in range(NS):
                    feed_forward(j, 2 * B + i * NS + j + 1)
                pe.wait_ge(a_th, B + (i + 1) * NS)

        @block.gpsimd
        def _(pool):
            nc.gpsimd.memset(ones[:, :], 1.0).then_inc(s_ones, 1)
            nc.gpsimd.memset(mhalf[:, :], -0.5).then_inc(s_ones, 1)
            nc.gpsimd.memset(v_s[:, :, :, :, HD:], 0.0).then_inc(s_ones, 1)
            pool.wait_ge(s_ones, 3)
            nc.gpsimd.memset(v_s[:, :, :, :, HD:HD + 1], 1.0).then_inc(s_ones, 1)

            def rsqrt(j, k, at):
                pool.wait_ge(a_var, at)
                nc.gpsimd.tensor_tensor(rstd[:, j, k, :], vare[:, j, k, :], mhalf[:, :], ALU.pow).then_inc(a_rstd, 1)

            with pool.Fori(0, B // NS) as i:
                for k in range(2):
                    for j in range(NS):
                        rsqrt(j, k, (i * 2 + k) * NS + j + 1)

            def k_sides(b, q):
                n = b * NQ + q
                pool.wait_ge(b_ks, n + 1)
                alone(pool, "pool")
                for sign, m in ((0, C_MPOS), (1, C_MNEG)):
                    for g in range(G):
                        last = nc.gpsimd.tensor_scalar(k_r[:, q % QPH, sign, g, :], ks[:, :],
                                                       cst[:, m + g:m + g + 1], 0.0, ALU.mult, ALU.add)
                last.then_inc(b_kr, 1)

            def row(b, last):
                for half in range(HALVES):
                    nb, nh = (b, 1) if half == 0 else (b + 1, 0)
                    if not (half == 1 and last):
                        for q in range(QPH * nh, QPH * (nh + 1)):
                            k_sides(nb, q)
            for q in range(QPH):
                k_sides(0, q)
            with pool.Fori(0, B - 1) as b:
                row(b, False)
            row(B - 1, True)

            with pool.Fori(0, B // NS) as i:
                for k in range(2):
                    for j in range(NS):
                        rsqrt(j, k, 2 * B + (i * 2 + k) * NS + j + 1)

        @block.scalar
        def _(act):
            act.wait_ge(s_wps, 1)
            act.activation(wvT[:, :], ps[:, 0, 0:P], ACT.Copy).then_inc(s_wsb, 1)
            act.activation(woT[:, :], ps[:, 0, P:2 * P], ACT.Copy).then_inc(s_wsb, 1)
            act.activation(w1T[:, :], ps[:, 0, 2 * P:3 * P], ACT.Copy).then_inc(s_wsb, 1)
            act.wait_ge(s_wps, 5)
            act.activation(w12T[:, :], ps[:, 7, 0:P], ACT.Copy).then_inc(s_wsb, 1)
            act.wait_ge(s_wps, 6)
            act.activation(wf[:, :], ps[:, 7, P:2 * P], ACT.Copy).then_inc(s_wsb, 1)
            act.wait_ge(s_setup, 1)

            def copy_transposed(dst, j, at):
                act.wait_ge(a_tp, at)
                act.activation(dst[j], ps[:, 2 * j, :].rearrange("p (t d) -> p t d", t=TC), ACT.Copy).then_inc(a_tcp, 1)

            def tanh(j, at):
                act.wait_ge(a_ff, at)
                act.activation(th[j], ps[:, 2 * j + 1, :].rearrange("p (t d) -> p t d", t=TC), ACT.Tanh).then_inc(a_th, 1)

            with act.Fori(0, B // NS) as i:
                for j in range(NS):
                    copy_transposed(xnT, j, i * 2 * NS + j + 1)
                for j in range(NS):
                    tanh(j, i * NS + j + 1)
                for j in range(NS):
                    copy_transposed(hTo, j, i * 2 * NS + NS + j + 1)
                act.wait_ge(a_sth, (i + 1) * NS * 16)

            act.sem_inc(b_sin, SET_CREDIT)

            def sines(b, half):
                for s in range(SETS_HALF):
                    m = s // SETS_PER_SINE
                    n = b * SETS_ROW + half * SETS_HALF + s
                    if s % SETS_PER_SINE == 0:
                        before = freed(m - SINS) if m >= SINS else freed(m - SINS + SINES_HALF) - ADDS_HALF
                        act.wait_ge(b_fma, b * ADDS_ROW + half * ADDS_HALF + before + SINE_CREDIT)
                    act.wait_ge(b_t, n + 1)
                    at = (s % SETS_PER_SINE) * SETS_PER_SINE * L
                    act.activation(sins[:, m % SINS, at:at + SETS_PER_SINE * L].rearrange("p (t l) -> p t l", l=L),
                                   ps[:, (s % SETS) * SETS_PER_SINE:(s % SETS + 1) * SETS_PER_SINE, :],
                                   ACT.Sin, scale=-TWO_PI_DOWN).then_inc(b_sin, 1)

            def sigmoids(b, half):
                for u in range(UNITS):
                    h = half * UNITS + u
                    act.wait_ge(b_fma, b * ADDS_ROW + half * ADDS_HALF + last_addition(u) + SINE_CREDIT)
                    act.activation(acc[:, u, :], acc[:, u, :], ACT.Sigmoid,
                                   scale=alpha_s[:, h, NF - 1:NF]).then_inc(b_sig, 1)

            def row(b, last):
                for half in range(HALVES):
                    sines(b, half)
                    sigmoids(b, half)
            with act.Fori(0, B - 1) as b:
                row(b, False)
            row(B - 1, True)

            with act.Fori(0, B // NS) as i:
                for j in range(NS):
                    copy_transposed(xnT, j, 2 * B + i * NS + j + 1)
                for j in range(NS):
                    tanh(j, B + i * NS + j + 1)
                act.wait_ge(c_st, (i + 1) * NS * 16)

        @block.vector
        def _(dve):
            dve.wait_ge(s_const, N_CONST * 16)
            steps = [0]

            def then_wait(ins):
                steps[0] += 1
                ins.then_inc(s_tab_step, 1)
                dve.wait_ge(s_tab_step, steps[0])

            then_wait(nc.vector.tensor_scalar(phit[:, :, :], phi4[:, :, :], float(1 / (2 * np.pi)), None, ALU.mult))
            dve.wait_ge(s_wps, 2)
            nc.vector.tensor_copy(wq_s[:, :, :], ps[:, 1:1 + NQ, 0:P])
            nc.vector.tensor_copy(wk_s[:, :, :], ps[:, 1:1 + NQ, P:2 * P])
            dve.wait_ge(s_wps, 3)
            nc.vector.tensor_copy(gb_bc[:, :, :], ps[:, 5, P:3 * P].rearrange("p (a n) -> p a n", a=2))
            then_wait(nc.vector.tensor_copy(alpha_bc[:, :], ps[:, 5, 0:H * NF + 1]))
            al = alpha_bc[:, 0:H * NF].rearrange("p (h f) -> p h f", h=H)
            then_wait(nc.vector.tensor_scalar(a_neg[:, :, :], al, 0.0, None, ALU.is_lt))
            then_wait(nc.vector.tensor_scalar(a_neg[:, :, :], a_neg[:, :, :], -2.0, 1.0, ALU.mult, ALU.add))
            then_wait(nc.vector.tensor_tensor(a_abs[:, :, :], al, a_neg[:, :, :], ALU.mult))
            then_wait(nc.vector.tensor_scalar(a_abs[:, :, :], a_abs[:, :, :], TINY, None, ALU.max))
            then_wait(nc.vector.tensor_tensor(alpha_s[:, :, :], a_abs[:, :, :], a_neg[:, :, :], ALU.mult))
            then_wait(nc.vector.reciprocal(a_neg[:, :, :], alpha_s[:, :, :]))
            then_wait(nc.vector.tensor_tensor(ratio[:, :, :], alpha_s[:, :, 0:NF - 1], a_neg[:, :, 1:NF], ALU.mult))
            temp = alpha_bc[:, H * NF:]
            then_wait(nc.vector.scalar_tensor_tensor(out=itemp[:, 0:1], in0=temp, scalar=-1.0, in1=temp,
                                                     op0=ALU.mult, op1=ALU.max))
            then_wait(nc.vector.tensor_scalar(itemp[:, 1:2], itemp[:, 0:1], 0.1, None, ALU.add))
            then_wait(nc.vector.reciprocal(itemp[:, 2:3], itemp[:, 1:2]))
            for f, freq in enumerate(FREQS):
                last = nc.vector.tensor_scalar(s_f[:, f:f + 1], itemp[:, 2:3], float(1 / (np.sqrt(HD) * freq)), None, ALU.mult)
            then_wait(last)
            then_wait(nc.vector.tensor_scalar(s_f[:, :], s_f[:, :], cst[:, C_QROW:C_QROW + 1], cst[:, C_MROW:C_MROW + 1],
                                              ALU.mult, ALU.add))
            dve.wait_ge(s_wps, 4)
            nc.vector.tensor_scalar(bq_c[:, :], ps[:, 6, 0:NQ], cst[:, C_ONE:C_ONE + 1], None, ALU.add)
            nc.vector.tensor_scalar(bk_c[:, :], ps[:, 6, NQ:2 * NQ], cst[:, C_ONE:C_ONE + 1], None, ALU.add)
            for q in range(NQ):
                last = nc.vector.tensor_tensor(s_tab[:, q, :], ps[:, 6, P + NF * q:P + NF * (q + 1)], s_f[:, :], ALU.add)
            then_wait(last)
            nc.vector.tensor_scalar(gs[:, :, :], s_tab[:, :, :], cst[:, C_QG:C_QG + 1], None, ALU.mult)
            then_wait(nc.vector.tensor_scalar(bs[:, :, :], s_tab[:, :, :], cst[:, C_QB:C_QB + 1], None, ALU.mult))
            dve.wait_ge(s_wsb, 5)
            dve.wait_ge(s_ones, 4)
            nc.vector.tensor_copy(itemp[:, 0:1], itemp[:, 1:2]).then_inc(s_setup, 1)

            def bank(j, k):
                return ps[:, 2 * j + k, :].rearrange("p (t d) -> p t d", t=TC)

            def moments(src, j, k, at):
                for t in range(TC):
                    last = nc.vector.bn_stats(out=stats[:, j, k, t, :], in_=src[:, t, :])
                last.then_inc(a_step, 1)
                dve.wait_ge(a_step, at + 1)
                alone(dve, "vector")
                for t in range(TC):
                    last = nc.vector.bn_aggr(out=mv[:, j, k, t, :], in_=stats[:, j, k, t, :])
                last.then_inc(a_step, 1)
                dve.wait_ge(a_step, at + 2)
                nc.vector.tensor_scalar(vare[:, j, k, :], mv[:, j, k, :, 1], EPS, None, ALU.add).then_inc(a_var, 1)

            def normalise(dst, src, j, k, at, done):
                dve.wait_ge(a_rstd, at)
                for t in range(TC):
                    last = nc.vector.tensor_scalar(dst[:, t, :], src[:, t, :], mv[:, j, k, t, 0:1], rstd[:, j, k, t:t + 1],
                                                   ALU.subtract, ALU.mult)
                last.then_inc(done, 1)

            A_STEPS = 4 * NS
            with dve.Fori(0, B // NS) as i:
                for j in range(NS):
                    dve.wait_ge(a_x[j], (i + 1) * 16)
                    moments(xin[j], j, 0, i * A_STEPS + 2 * j)
                for j in range(NS):
                    normalise(xn[j], xin[j], j, 0, i * 2 * NS + j + 1, a_norm)
                for j in range(NS):
                    dve.wait_ge(a_th, i * NS + j + 1)
                    nc.vector.scalar_tensor_tensor(out=x1t[j], in0=th[j], scalar=0.5, in1=xin[j],
                                                   op0=ALU.mult, op1=ALU.add).then_inc(a_x1, 1)
                    dve.wait_ge(a_x1, i * NS + j + 1)
                    moments(x1t[j], j, 1, i * A_STEPS + 2 * NS + 2 * j)
                for j in range(NS):
                    normalise(hn[j], x1t[j], j, 1, (i * 2 + 1) * NS + j + 1, a_norm)
                dve.wait_ge(a_stx, (i + 1) * NS * 16)

            dve.sem_inc(b_fma, SINE_CREDIT)
            STEPS_QUAD = 2 + 2 * (NF - 1)

            def split(b, q):
                n = b * NQ + q
                step = n * STEPS_QUAD
                slot = q % QPH
                dve.wait_ge(b_kps, n + 1)
                nc.vector.tensor_scalar(xk[:, q % 2, :], ps[:, BK_A, :], bk_c[:, q:q + 1], None, ALU.add).then_inc(b_xk, 1)
                dve.wait_ge(b_qps, n + 1)
                nc.vector.tensor_scalar(xq[:, :], ps[:, BK_B, :], bq_c[:, q:q + 1], None, ALU.add).then_inc(b_xq, 1)
                dve.wait_ge(b_xk, n + 1)
                nc.vector.tensor_scalar(hi_r[:, 0, :], xk[:, q % 2, :], cst[:, C_KG:C_KG + 1], None, ALU.mult).then_inc(b_step, 1)
                dve.wait_ge(b_xq, n + 1)
                nc.vector.tensor_scalar(hi_r[:, 1, :], xq[:, :], gs[:, q, 0:1], None, ALU.mult).then_inc(b_step, 1)
                dve.wait_ge(b_step, step + 1)
                dve.wait_ge(b_kr, n)
                nc.vector.scalar_tensor_tensor(out=ks[:, :], in0=xk[:, q % 2, :], scalar=cst[:, C_KB:C_KB + 1],
                                               in1=hi_r[:, 0, :].bitcast(F32), op0=ALU.mult, op1=ALU.subtract).then_inc(b_ks, 1)
                dve.wait_ge(b_ks, n + 1)
                for f in range(NF):
                    if f + 1 < NF:
                        nc.vector.tensor_scalar(hi_r[:, f % 2, :], xq[:, :], gs[:, q, f + 1:f + 2], None, ALU.mult).then_inc(b_step, 1)
                    dve.wait_ge(b_step, step + 2 + 2 * f)
                    last = nc.vector.scalar_tensor_tensor(out=q_r[:, slot, f, :], in0=xq[:, :], scalar=bs[:, q, f:f + 1],
                                                          in1=hi_r[:, (f + 1) % 2, :].bitcast(F32),
                                                          op0=ALU.mult, op1=ALU.subtract)
                    if f + 1 < NF:
                        last.then_inc(b_step, 1)
                        dve.wait_ge(b_step, step + 4 + 2 * f)
                last.then_inc(b_qr, 1)
                dve.wait_ge(b_vps, n + 1)
                nc.vector.tensor_copy(v_s[:, q, :, :, 0:HD],
                                      ps[:, BK_A, :].rearrange("p (t x) -> p t x", t=TC)[:, :, 0:R]
                                      .rearrange("p t (g d) -> p t g d", g=G)).then_inc(b_v, 1)

            def add_sines(b, half):
                base = b * ADDS_ROW + half * ADDS_HALF + SINE_CREDIT
                for m, (unit, f) in enumerate(order(half)):
                    q = half * QPH + unit // G
                    h = q * G + unit % G
                    dve.wait_ge(b_sin, b * SETS_ROW + half * SETS_HALF + SETS_PER_SINE * (m + 1) + SET_CREDIT)
                    if f == 0:
                        continue
                    if f == 1:
                        dve.wait_ge(b_pv, b * NQ + q - QPH + 1 + PV_CREDIT)
                        before = sins[:, (m - 2) % SINS, :]
                    else:
                        dve.wait_ge(b_fma, base + added(m) - 2)
                        before = acc[:, unit, :]
                    ins = nc.vector.scalar_tensor_tensor(out=acc[:, unit, :], in0=before, scalar=ratio[:, h, f - 1:f],
                                                         in1=sins[:, m % SINS, :], op0=ALU.mult, op1=ALU.add)
                    ins.then_inc(b_fma, 1)

            def copy_pv(b, q):
                n = b * NQ + q
                dve.wait_ge(b_st, n * STORES * 16 + STORE_CREDIT)
                dve.wait_ge(b_pv, n + 1 + PV_CREDIT)
                nc.vector.tensor_copy(o_sb[:, :], ps[:, BK_A, :]).then_inc(b_o, 1)

            dve.sem_inc(b_o, COPY_CREDIT)
            for q in range(QPH):
                split(0, q)

            def row(b, last):
                for half in range(HALVES):
                    add_sines(b, half)
                    nb, nh = (b, 1) if half == 0 else (b + 1, 0)
                    if not (half == 1 and last):
                        for q in range(QPH * nh, QPH * (nh + 1)):
                            split(nb, q)
                    for q in range(QPH * half, QPH * (half + 1)):
                        copy_pv(b, q)
            with dve.Fori(0, B - 1) as b:
                row(b, False)
            row(B - 1, True)

            C_STEPS = 5 * NS
            c0 = (B // NS) * A_STEPS
            dve.wait_ge(c_den, 16)
            nc.vector.tensor_scalar(den_a, den_a, 1e-10, None, ALU.add).then_inc(c_eps, 1)
            dve.wait_ge(c_eps, 1)
            nc.vector.reciprocal(den_a, den_a).then_inc(c_rden, 1)
            with dve.Fori(0, B // NS) as i:
                for j in range(NS):
                    dve.wait_ge(c_sp, i * NS + j + 1)
                    nc.vector.tensor_tensor(xin[j], xin[j], bank(j, 0), ALU.mult).then_inc(c_on, 1)
                for j in range(NS):
                    dve.wait_ge(c_y, i * NS + j + 1)
                    nc.vector.tensor_copy(yv[j], bank(j, 1)).then_inc(a_step, 1)
                    dve.wait_ge(a_step, c0 + i * C_STEPS + 3 * j + 1)
                    moments(yv[j], j, 0, c0 + i * C_STEPS + 3 * j + 1)
                for j in range(NS):
                    at = i * NS + j
                    normalise(hn[j], yv[j], j, 0, 2 * B + i * 2 * NS + j + 1, c_y2)
                    dve.wait_ge(c_y2, at * 4 + 1)
                    nc.vector.tensor_tensor(hn[j], hn[j], gb_bc[:, 0:1, :].to_broadcast([P, TC, D]), ALU.mult).then_inc(c_y2, 1)
                    dve.wait_ge(c_y2, at * 4 + 2)
                    nc.vector.tensor_tensor(hn[j], hn[j], gb_bc[:, 1:2, :].to_broadcast([P, TC, D]), ALU.add).then_inc(c_y2, 1)
                    dve.wait_ge(c_y2, at * 4 + 3)
                    dve.wait_ge(c_ld[j], (i + 1) * 48)
                    nc.vector.tensor_tensor(x1t[j], hn[j], x1t[j], ALU.add).then_inc(c_y2, 1)
                    dve.wait_ge(c_y2, at * 4 + 4)
                    moments(x1t[j], j, 1, c0 + i * C_STEPS + 3 * NS + 2 * j)
                for j in range(NS):
                    normalise(xn[j], x1t[j], j, 1, 2 * B + (i * 2 + 1) * NS + j + 1, a_norm)
                for j in range(NS):
                    dve.wait_ge(a_th, B + i * NS + j + 1)
                    nc.vector.scalar_tensor_tensor(out=th[j], in0=th[j], scalar=0.5, in1=x1t[j],
                                                   op0=ALU.mult, op1=ALU.add).then_inc(c_out, 1)


NAMES = ['L0_attn_x', 'L0_attn_Wq', 'L0_attn_bq', 'L0_attn_Wk', 'L0_attn_bk', 'L0_attn_Wv', 'L0_attn_bv',
         'L0_attn_Wo', 'L0_attn_bo', 'L0_attn_alpha', 'L0_attn_phi', 'L0_attn_temperature', 'L0_attn_gamma',
         'L0_attn_beta', 'L0_ffn_weight', 'L0_ffn_aux_weight1', 'L0_ffn_aux_weight2', 'L0_ffn_bias']


def kernel(**inputs):
    import concourse.bacc as bacc
    from concourse.bass_utils import run_bass_kernel_spmd

    nc = bacc.Bacc("TRN2", target_bir_lowering=False, num_devices=1)
    arrays, args = {}, []
    for name in NAMES:
        a = np.ascontiguousarray(inputs[name])
        arrays[f"in_{name}"] = a
        args.append(nc.dram_tensor(f"in_{name}", a.shape, mybir.dt.from_np(a.dtype), kind="ExternalInput").ap())
    c = constants()
    arrays["in_consts"] = c
    args.append(nc.dram_tensor("in_consts", c.shape, mybir.dt.float32, kind="ExternalInput").ap())
    args.append(nc.dram_tensor("out", (B, L, D), mybir.dt.float32, kind="ExternalOutput").ap())
    build(nc, *args)
    r = run_bass_kernel_spmd(nc, [arrays], core_ids=[0])
    return r.results[0]["out"]
```

```python
import numpy as np
import concourse.bass as bass
from concourse import mybir
from contextlib import ExitStack

B, L, D = 16, 512, 128
H, HD = 16, 8
FREQS = (31.0, 37.0, 41.0, 43.0, 47.0)
NF = len(FREQS)
P = 128
TC = L // P
G = 4
NQ = H // G
R = P // G
HALVES = 2
QPH = NQ // HALVES
UNITS = QPH * G
SINS = 5
SETS = 3
SETS_PER_SINE = 2
MAGIC = 1.5 * 2.0 ** 23
TWO_PI_DOWN = float(np.nextafter(np.float32(2 * np.pi), np.float32(0)))
EPS = 1e-5
TINY = 1e-18

C_IDENT, C_HEADS, C_REP, C_PHIREP = 0, 128, 256, 384
C_QG, C_QB, C_KG, C_KB, C_KNEG, C_MROW, C_QROW, C_ONE = range(512, 520)
NCONST = 520


def constants():
    c = np.zeros((P, NCONST), np.float32)
    c[:, C_IDENT:C_IDENT + P] = np.eye(P)
    r = np.arange(P) % R
    for k in range(H):
        c[k, C_HEADS + HD * k:C_HEADS + HD * (k + 1)] = 1.0
    for k in range(P):
        head, d = (k % R) // HD, k % HD
        for part in range(3):
            c[k, C_REP + R * head + HD * part + d] = 1.0
    for k in range(G):
        c[k, C_PHIREP + R * k + 24:C_PHIREP + R * k + 26] = 1.0
    q_low = (r < 8) | (r == 25)
    k_low = (r >= 8) & (r < 16)
    c[:, C_QG], c[:, C_QB] = np.where(q_low, 1, -1), np.where(q_low, 1, 0)
    c[:, C_KG], c[:, C_KB] = np.where(k_low, 1, -1), np.where(k_low, 1, 0)
    c[:, C_KNEG] = -1.0 * (r < 26)
    c[:, C_MROW] = np.where(r == 26, MAGIC, np.where(r == 27, -MAGIC, 0))
    c[:, C_QROW] = r < 24
    c[:, C_ONE] = (r >= 24) & (r < 28)
    return c


def build(nc, x, Wq, bq, Wk, bk, Wv, bv, Wo, bo, alpha, phi, temperature, gamma, beta,
          W1, W2, W3, bias, consts, out):
    F32, F32R = mybir.dt.float32, mybir.dt.float32r
    ALU, ACT = mybir.AluOpType, mybir.ActivationFunctionType
    ctx = ExitStack()
    with ctx:
        def sb(name, shape, dt=F32):
            return ctx.enter_context(nc.sbuf_tensor(name, shape, dt))

        def sem(name):
            return ctx.enter_context(nc.semaphore(name))

        x1_d = nc.dram_tensor("x1_scratch", (B, P, TC, D), F32).ap()
        hT_d = nc.dram_tensor("hT_scratch", (B, D, L), F32).ap()
        oT_d = nc.dram_tensor("oT_scratch", (B, D, L), F32).ap()
        den_d = nc.dram_tensor("den_scratch", (B, H, L), F32).ap()
        rden_d = nc.dram_tensor("rden_scratch", (B, H, L), F32).ap()

        cst = sb("cst", [P, NCONST])
        ident = cst[:, C_IDENT:C_IDENT + P]
        wq_s = sb("wq_s", [P, NQ, P])
        wk_s = sb("wk_s", [P, NQ, P])
        wvT = sb("wvT", [P, P])
        woT = sb("woT", [P, P])
        w1T = sb("w1T", [P, P])
        w12T = sb("w12T", [P, P])
        wf = sb("wf", [P, P])
        rows = sb("rows", [1, 5, P])
        misc = sb("misc", [1, H * NF + 1])
        bqk = sb("bqk", [R, 2, NQ])
        phi4 = sb("phi4", [G, NQ, NF])
        phit = sb("phit", [G, NQ, NF])
        ones = sb("ones", [P, P])
        alpha_bc = sb("alpha_bc", [P, H * NF + 1])
        a_neg = sb("a_neg", [P, H, NF])
        a_abs = sb("a_abs", [P, H, NF])
        alpha_s = sb("alpha_s", [P, H, NF])
        ratio = sb("ratio", [P, H, NF - 1])
        gb_bc = sb("gb_bc", [P, 2, P])
        bq_c = sb("bq_c", [P, NQ])
        bk_c = sb("bk_c", [P, NQ])
        itemp = sb("itemp", [P, 3])
        s_f = sb("s_f", [P, NF])
        s_tab = sb("s_tab", [P, NQ, NF])
        gs = sb("gs", [P, NQ, NF])
        bs = sb("bs", [P, NQ, NF])
        mhalf = sb("mhalf", [P, TC])

        sins = sb("sins", [P, SINS, TC * L])
        acc = sb("acc", [P, UNITS, TC * L])
        q_r = sb("q_r", [P, QPH, NF, L], F32R)
        k_r = sb("k_r", [P, QPH, 2, G, L], F32R)
        hi_r = sb("hi_r", [P, 3, L], F32R)
        xq = sb("xq", [P, L])
        xk = sb("xk", [P, L])
        ks = sb("ks", [P, QPH, 2, L], F32R)
        v_s = sb("v_s", [P, TC, H, R])
        bv_bc = sb("bv_bc", [P, P])
        hT = sb("hT", [P, L])
        o_sb = sb("o_sb", [P, QPH, L])
        den_a = sins[:, 0, 0:B * H * L // P]
        wnat = sins[:, 0, 0:7 * P].rearrange("p (w n) -> p w n", w=7)

        NS = 4

        def tile(k):
            return [acc[:, k, L * j:L * (j + 1)].rearrange("p (t d) -> p t d", t=TC) for j in range(NS)]

        xin, xn, xnT, th, x1t, hn, hTo, yv = (tile(k) for k in range(UNITS))
        rd16 = [sins[0:H, 1, L * j:L * (j + 1)] for j in range(NS)]
        stats = sb("stats", [P, NS, 2, TC, 6])
        mv = sb("mv", [P, NS, 2, TC, 2])
        vare = sb("vare", [P, NS, 2, TC])
        nmean = sb("nmean", [P, NS, 2, TC])
        rstd = sb("rstd", [P, NS, 2, TC])
        nmr = sb("nmr", [P, NS, 2, TC])

        ps = ctx.enter_context(nc.psum_tensor("ps", [P, 8, L], F32))
        BK_A, BK_B = 6, 7
        KQ_BANKS = ((BK_A, BK_B), (2 * SETS - 2, 2 * SETS - 1))

        s_const = sem("consts_loaded")
        s_ones = sem("ones_set")
        s_wps = sem("setup_product_ready")
        s_wsb = sem("setup_product_copied")
        s_tab_step = sem("setup_table_step")
        s_setup = sem("setup_done")
        m_stats = [sem(f"ac_stats_{k}") for k in range(4)]
        m_mv = [sem(f"ac_mean_and_variance_{k}") for k in range(4)]
        m_var = [sem(f"ac_guarded_variance_{k}") for k in range(4)]
        m_rstd = [sem(f"ac_rstd_{k}") for k in range(4)]
        m_nmr = [sem(f"ac_shift_{k}") for k in range(4)]
        a_x = [sem(f"a_x_loaded_{j}") for j in range(NS)]
        a_n1 = sem("a_x_normalised")
        a_t1 = sem("a_x_transposed_in_psum")
        a_c1 = sem("a_x_transposed_in_sbuf")
        a_ff = sem("a_ffn_in_psum")
        a_th = sem("a_tanh_ready")
        a_x1 = sem("a_x1_ready")
        a_n2 = sem("a_x1_normalised")
        a_t2 = sem("a_x1_transposed_in_psum")
        a_c2 = sem("a_x1_transposed_in_sbuf")
        a_stx = [sem(f"a_x1_stored_{j}") for j in range(NS)]
        a_sth = [sem(f"a_hT_stored_{j}") for j in range(NS)]
        b_h = sem("b_hT_loaded")
        b_kps = sem("b_k_in_psum")
        b_qps = sem("b_q_in_psum")
        b_vps = sem("b_v_in_psum")
        b_xk = sem("b_k_biased")
        b_xq = sem("b_q_biased")
        b_v = sem("b_v_copied")
        b_step = sem("b_vector_split_step")
        b_kp = sem("b_k_split")
        b_ks = sem("b_k_negated")
        b_kr = [sem(f"b_k_sides_ready_{slot}") for slot in range(QPH)]
        b_qr = sem("b_q_sides_ready")
        b_t = sem("b_angles_ready")
        b_sin = sem("b_sines_ready")
        b_fma = sem("b_sine_added")
        b_sig = sem("b_sigmoids_ready")
        b_pv = sem("b_pv_in_psum")
        b_o = sem("b_pv_copied")
        b_st = [sem(f"b_heads_stored_{slot}") for slot in range(QPH)]
        c_den = sem("c_denominators_moved")
        c_eps = sem("c_denominators_guarded")
        c_rden = sem("c_reciprocals_ready")
        c_lo = [sem(f"c_heads_loaded_{j}") for j in range(NS)]
        c_lx = [sem(f"c_x1_loaded_{j}") for j in range(NS)]
        c_sp = sem("c_reciprocals_in_psum")
        c_on = sem("c_heads_normalised")
        c_y = sem("c_projection_in_psum")
        c_xb = sem("c_beta_added")
        c_yn = sem("c_projection_normalised")
        c_yg = sem("c_times_gamma")
        c_x2 = sem("c_attention_added")
        c_n = sem("c_x2_normalised")
        c_t = sem("c_x2_transposed_in_psum")
        c_c = sem("c_x2_transposed_in_sbuf")
        c_ff = sem("c_ffn_in_psum")
        c_th = sem("c_tanh_ready")
        c_out = sem("c_out_ready")
        c_st = [sem(f"c_out_stored_{j}") for j in range(NS)]

        N_CONST = 18

        s_passed = {name: sem(f"waits_passed_by_{name}") for name in ("sync", "pool", "vector")}

        def alone(eng, name):
            eng.sem_inc(s_passed[name], 1)

        ROW_CREDIT, DMA_CREDIT = NS, 16

        def by_token(bank):
            return ps[:, bank, :].rearrange("p (t d) -> p t d", t=TC)

        def A_TR(j): return 2 * j
        def A_FF(j): return 2 * j + 1
        def C_SP(j): return j % 2
        def C_Y(j): return 2 + j
        def C_TR(j): return 6
        def C_FF(j): return 7

        def pipelined(eng, stages):
            peeled = max(1, -(-max(lag for lag, _ in stages) // NS))
            for step in range(peeled * NS):
                for lag, work in stages:
                    if step >= lag:
                        work(step - lag, (step - lag) // NS, (step - lag) % NS)
            with eng.Fori(peeled, B // NS) as i:
                for j in range(NS):
                    for lag, work in stages:
                        work(i * NS + (j - lag), i + (j - lag) // NS, (j - lag) % NS)
            for step in range(B, B + max(lag for lag, _ in stages)):
                for lag, work in stages:
                    if step - lag < B:
                        work(step - lag, (step - lag) // NS, (step - lag) % NS)

        block = ctx.enter_context(nc.Block())

        SETS_HALF = UNITS * NF * SETS_PER_SINE
        SETS_ROW = HALVES * SETS_HALF
        AFTER_LAST_SET = (SETS_HALF - SETS) % SETS
        SINES_HALF = UNITS * NF
        UNITS_ROW = HALVES * UNITS
        SET_CREDIT, SINE_CREDIT, PV_CREDIT, COPY_CREDIT = SETS, SINS, QPH, 1
        STORES = G + 1
        STORE_CREDIT = 16

        def order(half):
            return [(2 * pair + a, f) for pair in range(UNITS // 2) for f in range(NF) for a in range(2)]

        ADDS_HALF = UNITS * (NF - 1)
        ADDS_ROW = HALVES * ADDS_HALF

        def added(m):
            return len([f for _, f in order(0)[:m + 1] if f > 0])

        def last_addition(unit):
            return added(max(m for m, (u, f) in enumerate(order(0)) if u == unit))

        def freed(m):
            return added(m + 2 if order(0)[m][1] == 0 else m)

        @block.sync
        def _(sp):
            sp.dma_start(cst[:, :], consts).then_inc(s_const, 16)
            for n, w in enumerate((Wq, Wk, Wv, Wo, W1, W2, W3)):
                sp.dma_start(wnat[:, n, :], w).then_inc(s_const, 16)
            for n, v in enumerate((bv, bo, bias, gamma, beta)):
                sp.dma_start(rows[0:1, n, :], v.rearrange("(a n) -> a n", a=1)).then_inc(s_const, 16)
            sp.dma_start(misc[0:1, 0:H * NF], alpha.rearrange("(a h) f -> a (h f)", a=1)).then_inc(s_const, 16)
            sp.dma_start(misc[0:1, H * NF:], temperature.rearrange("(a n) -> a n", a=1)).then_inc(s_const, 16)
            sp.dma_start(phi4[:, :, :], phi.rearrange("(q g) f -> g q f", g=G)).then_inc(s_const, 16)

            sp.dma_start(bqk[:, 0, :], bq.rearrange("(q p) -> p q", p=R), allow_slow_non_contiguous=True).then_inc(s_const, 16)
            sp.dma_start(bqk[:, 1, :], bk.rearrange("(q p) -> p q", p=R), allow_slow_non_contiguous=True).then_inc(s_const, 16)

            for j in range(NS):
                sp.sem_inc(a_stx[j], DMA_CREDIT)
                sp.sem_inc(a_sth[j], DMA_CREDIT)
            sp.sem_inc(a_x1, ROW_CREDIT)

            def load_x(row, turn, j):
                sp.wait_ge(a_x1, row + 1)
                alone(sp, "sync")
                sp.dma_start(xin[j], x[bass.ds(row, 1)].rearrange("o (p t) d -> p (o t) d", t=TC)).then_inc(a_x[j], 16)

            def store_x1(row, turn, j):
                sp.wait_ge(a_x1, row + 1 + ROW_CREDIT)
                alone(sp, "sync")
                sp.dma_start(x1_d[bass.ds(row, 1)].rearrange("o p t d -> p (o t) d"), x1t[j]).then_inc(a_stx[j], 16)

            def store_hT(row, turn, j):
                sp.wait_ge(a_c2, row + 1)
                alone(sp, "sync")
                sp.dma_start(hT_d[bass.ds(row, 1)].rearrange("o d l -> d (o l)"),
                             hTo[j].rearrange("p t d -> p (t d)")).then_inc(a_sth[j], 16)

            pipelined(sp, ((0, load_x), (4, store_x1), (6, store_hT)))
            for j in range(NS):
                sp.wait_ge(a_stx[j], B // NS * 16 + DMA_CREDIT)
                sp.wait_ge(a_sth[j], B // NS * 16 + DMA_CREDIT)

            for slot in range(QPH):
                sp.sem_inc(b_st[slot], STORE_CREDIT)
            sp.dma_start(hT[:, :], hT_d[0]).then_inc(b_h, 16)

            def k_sides(i, q):
                sp.wait_ge(b_ks, i * NQ + q + 1)
                alone(sp, "sync")
                for g in range(G):
                    rows_g = slice(R * g, R * (g + 1))
                    sp.dma_start(k_r[rows_g, q % QPH, :, g, :].bitcast(F32), ks[rows_g, q % QPH, :, :].bitcast(F32)).then_inc(b_kr[q % QPH], 16)

            def store_heads(i, q):
                sp.wait_ge(b_o, i * NQ + q + 1 + COPY_CREDIT)
                alone(sp, "sync")
                for g in range(G):
                    sp.dma_start(oT_d[bass.ds(i, 1), (q * G + g) * HD:(q * G + g + 1) * HD, :].rearrange("o d l -> d (o l)"),
                                 o_sb[R * g:R * g + HD, q % QPH, :]).then_inc(b_st[q % QPH], 16)
                sp.dma_start(den_d[bass.ds(i, 1), q * G:(q + 1) * G, :].rearrange("o h l -> h (o l)"),
                             o_sb[HD:HD + R * (G - 1) + 1:R, q % QPH, :]).then_inc(b_st[q % QPH], 16)

            def row(i, last):
                for half in range(HALVES):
                    ni, nh = (i, 1) if half == 0 else (i + 1, 0)
                    if not (half == 1 and last):
                        for q in range(QPH * nh, QPH * (nh + 1)):
                            k_sides(ni, q)
                    if half == 0 and not last:
                        sp.wait_ge(b_qps, i * NQ + NQ)
                        alone(sp, "sync")
                        sp.dma_start(hT[:, :], hT_d[bass.ds(i + 1, 1)].rearrange("o d l -> d (o l)")).then_inc(b_h, 16)
                    for q in range(QPH * half, QPH * (half + 1)):
                        store_heads(i, q)
            for q in range(QPH):
                k_sides(0, q)
            with sp.Fori(0, B - 1) as i:
                row(i, False)
            row(B - 1, True)
            for slot in range(QPH):
                sp.wait_ge(b_st[slot], B * HALVES * STORES * 16 + STORE_CREDIT)
            sp.dma_start(den_a[:, :], den_d.rearrange("b h (s l) -> (b h s) l", s=1).rearrange("(p r) l -> p (r l)", p=P)).then_inc(c_den, 16)
            sp.wait_ge(c_rden, 1)
            sp.dma_start(rden_d.rearrange("b h l -> (b h) l").rearrange("(p r) l -> p (r l)", p=P), den_a[:, :]).then_inc(c_den, 16)
            sp.wait_ge(c_den, 32)

            for j in range(NS):
                sp.sem_inc(c_st[j], DMA_CREDIT)
            sp.sem_inc(c_y, ROW_CREDIT)
            sp.sem_inc(c_xb, ROW_CREDIT)

            def load_heads(row, turn, j):
                sp.wait_ge(c_y, row + 1)
                alone(sp, "sync")
                sp.dma_start(xin[j].rearrange("p t d -> p (t d)"),
                             oT_d[bass.ds(row, 1)].rearrange("o d l -> d (o l)")).then_inc(c_lo[j], 16)
                sp.dma_start(rd16[j], rden_d[bass.ds(row, 1)].rearrange("o h l -> h (o l)")).then_inc(c_lo[j], 16)

            def load_x1(row, turn, j):
                sp.wait_ge(c_xb, row + 1)
                alone(sp, "sync")
                sp.dma_start(x1t[j], x1_d[bass.ds(row, 1)].rearrange("o p t d -> p (o t) d")).then_inc(c_lx[j], 16)

            def store_out(row, turn, j):
                sp.wait_ge(c_out, row + 1)
                alone(sp, "sync")
                sp.dma_start(out[bass.ds(row, 1)].rearrange("o (p t) d -> p (o t) d", t=TC), th[j]).then_inc(c_st[j], 16)

            pipelined(sp, ((0, load_heads), (1, load_x1), (8, store_out)))
            for j in range(NS):
                sp.wait_ge(c_st[j], B // NS * 16 + DMA_CREDIT)

        @block.tensor
        def _(pe):
            pe.wait_ge(s_const, N_CONST * 16)
            pe.wait_ge(s_ones, 1)
            one = ones[0:1, 0:P]
            nc.tensor.transpose(ps[:, 0, 0:P], wnat[:, 2, :], ident)
            nc.tensor.transpose(ps[:, 0, P:2 * P], wnat[:, 3, :], ident)
            nc.tensor.transpose(ps[:, 0, 2 * P:3 * P], wnat[:, 4, :], ident).then_inc(s_wps, 1)
            for q in range(NQ):
                rep = slice(R * q, R * (q + 1))
                for n in range(2):
                    mm = nc.tensor.matmul(ps[:, 1 + q, P * n:P * (n + 1)], wnat[rep, n, :],
                                          cst[rep, C_REP:C_REP + P], start=True, stop=True)
            mm.then_inc(s_wps, 1)
            nc.tensor.matmul(ps[:, 5, 0:H * NF + 1], one, misc[0:1, :], start=True, stop=True)
            nc.tensor.matmul(ps[:, 5, P:P + 2 * P], one, rows[0:1, 3:5, :], start=True, stop=True)
            nc.tensor.matmul(ps[:, 5, 3 * P:4 * P], one, rows[0:1, 0, :], start=True, stop=True).then_inc(s_wps, 1)
            nc.tensor.matmul(ps[:, 6, 0:2 * NQ], cst[0:R, C_REP:C_REP + P], bqk[:, :, :], start=True, stop=True)
            pe.wait_ge(s_tab_step, 1)
            nc.tensor.matmul(ps[:, 6, P:P + NQ * NF], cst[0:G, C_PHIREP:C_PHIREP + P], phit[:, :, :],
                             start=True, stop=True).then_inc(s_wps, 1)
            pe.wait_ge(s_wsb, 3)
            nc.tensor.matmul(ps[:, 7, 0:P], wnat[:, 5, :], w1T[:, :], start=True, stop=True).then_inc(s_wps, 1)
            pe.wait_ge(s_wsb, 4)
            nc.tensor.matmul(ps[:, 7, P:2 * P], w12T[:, :], wnat[:, 6, :], start=True, stop=True).then_inc(s_wps, 1)
            pe.wait_ge(s_setup, 1)

            def transposes(src, bank, ready, done):
                def work(row, turn, j):
                    pe.wait_ge(ready, row + 1)
                    for t in range(TC):
                        mm = nc.tensor.transpose(ps[:, bank(j), P * t:P * (t + 1)], src[j][:, t, :], ident)
                    mm.then_inc(done, 1)
                return work

            def feed_forward(bank, ready, done):
                def work(row, turn, j):
                    pe.wait_ge(ready, row + 1)
                    for t in range(TC):
                        o = ps[:, bank(j), P * t:P * (t + 1)]
                        nc.tensor.matmul(o, xnT[j][:, t, :], wf[:, :], start=True, stop=False)
                        mm = nc.tensor.matmul(o, one, rows[0:1, 2, :], start=False, stop=True)
                    mm.then_inc(done, 1)
                return work

            pipelined(pe, ((2, feed_forward(A_FF, a_c1, a_ff)),
                           (1, transposes(xn, A_TR, a_n1, a_t1)),
                           (4, transposes(hn, A_TR, a_n2, a_t2))))

            def project(b, q, first=False):
                n = b * NQ + q
                if q % QPH == 0:
                    if q == 0:
                        pe.wait_ge(b_h, (b + 1) * 16)
                    else:
                        pe.wait_ge(b_v, b + 1)
                    if not first:
                        pe.wait_ge(b_o, n - QPH + COPY_CREDIT)
                elif not first:
                    pe.wait_ge(b_sin, b * SETS_ROW + (q // QPH) * SETS_HALF - AFTER_LAST_SET + SET_CREDIT)
                k_bank, q_bank = KQ_BANKS[q % QPH]
                nc.tensor.matmul(ps[:, k_bank, :], wk_s[:, q, :], hT[:, :], start=True, stop=True).then_inc(b_kps, 1)
                nc.tensor.matmul(ps[:, q_bank, :], wq_s[:, q, :], hT[:, :], start=True, stop=True).then_inc(b_qps, 1)

            def values():
                for t in range(TC):
                    mm = nc.tensor.matmul(ps[:, BK_A, P * t:P * (t + 1)], hT[:, P * t:P * (t + 1)], wvT[:, :],
                                          start=True, stop=True)
                mm.then_inc(b_vps, 1)

            def angles(b, half, lo, hi):
                for s in range(lo, hi):
                    unit, f = order(half)[s // SETS_PER_SINE]
                    slot, g = unit // G, unit % G
                    n = b * SETS_ROW + half * SETS_HALF + s
                    if s < SETS:
                        if s == 0:
                            pe.wait_ge(b_sin, b * SETS_ROW + half * SETS_HALF + SET_CREDIT)
                    else:
                        pe.wait_ge(b_sin, n - SETS + 1 + SET_CREDIT)
                    if s == SETS - 1:
                        pe.wait_ge(b_xk, b * NQ + half * QPH + QPH)
                        pe.wait_ge(b_xq, b * NQ + half * QPH + QPH)
                    if s == 0 or s == G * NF * SETS_PER_SINE:
                        pe.wait_ge(b_kr[slot], (b * HALVES + half + 1) * G * 16)
                        pe.wait_ge(b_qr, b * NQ + half * QPH + slot + 1)
                    for t in range(SETS_PER_SINE):
                        block_at = (s % SETS_PER_SINE) * SETS_PER_SINE + t
                        keys = slice(P * block_at, P * (block_at + 1))
                        o = ps[:, (s % SETS) * SETS_PER_SINE + t, :]
                        nc.tensor.matmul(o, k_r[:, slot, 0, g, keys], q_r[:, slot, f, :], start=True, stop=False)
                        mm = nc.tensor.matmul(o, k_r[:, slot, 1, g, keys], q_r[:, slot, f, :], start=False, stop=True)
                    mm.then_inc(b_t, 1)

            def attend(b, q, last=False):
                bank, read = ((BK_A, b_xk), (BK_B, b_xq))[q % QPH]
                if not last:
                    pe.wait_ge(read, b * NQ + (q // QPH + 1) * QPH + 1)
                pe.wait_ge(b_sig, b * UNITS_ROW + G * (q + 1))
                for t in range(TC):
                    for g in range(G):
                        mm = nc.tensor.matmul(ps[R * g:R * (g + 1), bank, :], v_s[:, t, q * G + g, :],
                                              acc[:, (q % QPH) * G + g, L * t:L * (t + 1)],
                                              start=(t == 0), stop=(t == TC - 1))
                mm.then_inc(b_pv, 1)

            AHEAD = SETS
            pe.sem_inc(b_pv, PV_CREDIT)
            for q in range(QPH):
                project(0, q, first=True)
            pe.wait_ge(b_xk, 1)
            values()
            angles(0, 0, 0, AHEAD)

            def row(b, last):
                for half in range(HALVES):
                    end = last and half == 1
                    nb, nh = (b, 1) if half == 0 else (b + 1, 0)
                    q0 = QPH * half
                    angles(b, half, AHEAD, SETS_HALF)
                    if not end:
                        for q in range(QPH * nh, QPH * (nh + 1)):
                            project(nb, q)
                    attend(b, q0, end)
                    if not end:
                        angles(nb, nh, 0, AHEAD)
                    attend(b, q0 + 1, end)
                    if half == 1 and not end:
                        pe.wait_ge(b_o, b * NQ + q0 + 1 + COPY_CREDIT)
                        values()
            with pe.Fori(0, B - 1) as b:
                row(b, False)
            row(B - 1, True)

            def spread(row, turn, j):
                pe.wait_ge(c_lo[j], (turn + 1) * 32)
                nc.tensor.matmul(ps[:, C_SP(j), :], cst[0:H, C_HEADS:C_HEADS + P], rd16[j], start=True, stop=True).then_inc(c_sp, 1)

            def output_projection(row, turn, j):
                pe.wait_ge(c_on, row + 1)
                for t in range(TC):
                    o = ps[:, C_Y(j), P * t:P * (t + 1)]
                    nc.tensor.matmul(o, xin[j][:, t, :], woT[:, :], start=True, stop=False)
                    mm = nc.tensor.matmul(o, one, rows[0:1, 1, :], start=False, stop=True)
                mm.then_inc(c_y, 1)

            pipelined(pe, ((5, feed_forward(C_FF, c_c, c_ff)), (1, output_projection), (0, spread),
                           (4, transposes(xn, C_TR, c_n, c_t))))

        @block.gpsimd
        def _(pool):
            nc.gpsimd.memset(ones[:, :], 1.0).then_inc(s_ones, 1)
            nc.gpsimd.memset(mhalf[:, :], -0.5).then_inc(s_ones, 1)
            nc.gpsimd.memset(v_s[:, :, :, HD:], 0.0).then_inc(s_ones, 1)
            nc.gpsimd.memset(k_r[:, :, :, :, :].bitcast(F32), 0.0).then_inc(s_ones, 1)
            pool.wait_ge(s_ones, 4)
            nc.gpsimd.memset(v_s[:, :, :, HD:HD + 1], 1.0).then_inc(s_ones, 1)

            def rsqrt(k):
                def work(row, turn, j):
                    pool.wait_ge(m_var[k], row + 1)
                    nc.gpsimd.tensor_tensor(rstd[:, j, k % 2, :], vare[:, j, k % 2, :], mhalf[:, :], ALU.pow).then_inc(m_rstd[k], 1)
                    pool.wait_ge(m_rstd[k], row + 1)
                    nc.gpsimd.tensor_tensor(nmr[:, j, k % 2, :], nmean[:, j, k % 2, :], rstd[:, j, k % 2, :], ALU.mult).then_inc(m_nmr[k], 1)
                return work

            pipelined(pool, ((3, rsqrt(1)), (0, rsqrt(0))))

            def add_beta(row, turn, j):
                pool.wait_ge(c_lx[j], (turn + 1) * 16)
                nc.gpsimd.tensor_tensor(hn[j], x1t[j], gb_bc[:, 1:2, :].to_broadcast([P, TC, D]), ALU.add).then_inc(c_xb, 1)

            pipelined(pool, ((2, add_beta), (2, rsqrt(2)), (3, rsqrt(3))))

        @block.scalar
        def _(act):
            act.wait_ge(s_wps, 1)
            act.activation(wvT[:, :], ps[:, 0, 0:P], ACT.Copy).then_inc(s_wsb, 1)
            act.activation(woT[:, :], ps[:, 0, P:2 * P], ACT.Copy).then_inc(s_wsb, 1)
            act.activation(w1T[:, :], ps[:, 0, 2 * P:3 * P], ACT.Copy).then_inc(s_wsb, 1)
            act.wait_ge(s_wps, 5)
            act.activation(w12T[:, :], ps[:, 7, 0:P], ACT.Copy).then_inc(s_wsb, 1)
            act.wait_ge(s_wps, 6)
            act.activation(wf[:, :], ps[:, 7, P:2 * P], ACT.Copy).then_inc(s_wsb, 1)
            act.wait_ge(s_setup, 1)

            def normalise(dst, src, k, done):
                def work(row, turn, j):
                    act.wait_ge(m_nmr[k], row + 1)
                    for t in range(TC):
                        last = act.activation(dst[j][:, t, :], src(j)[:, t, :], ACT.Identity,
                                              bias=nmr[:, j, k % 2, t:t + 1], scale=rstd[:, j, k % 2, t:t + 1])
                    last.then_inc(done, 1)
                return work

            def copy_transposed(dst, bank, ready, done, stored=None):
                def work(row, turn, j):
                    if stored:
                        act.wait_ge(stored[j], turn * 16 + DMA_CREDIT)
                    act.wait_ge(ready, row + 1)
                    act.activation(dst[j], by_token(bank(j)), ACT.Copy).then_inc(done, 1)
                return work

            def tanh(bank, ready, done, stored=None):
                def work(row, turn, j):
                    if stored:
                        act.wait_ge(stored[j], turn * 16 + DMA_CREDIT)
                    act.wait_ge(ready, row + 1)
                    act.activation(th[j], by_token(bank(j)), ACT.Tanh).then_inc(done, 1)
                return work

            pipelined(act, ((1, normalise(xn, lambda j: xin[j], 0, a_n1)),
                            (4, normalise(hn, lambda j: x1t[j], 1, a_n2)),
                            (2, tanh(A_FF, a_ff, a_th)),
                            (1, copy_transposed(xnT, A_TR, a_t1, a_c1)),
                            (4, copy_transposed(hTo, A_TR, a_t2, a_c2, a_sth))))

            act.sem_inc(b_sin, SET_CREDIT)

            def sines(b, half):
                for s in range(SETS_HALF):
                    m = s // SETS_PER_SINE
                    n = b * SETS_ROW + half * SETS_HALF + s
                    if s % SETS_PER_SINE == 0:
                        before = freed(m - SINS) if m >= SINS else freed(m - SINS + SINES_HALF) - ADDS_HALF
                        act.wait_ge(b_fma, b * ADDS_ROW + half * ADDS_HALF + before + SINE_CREDIT)
                    act.wait_ge(b_t, n + 1)
                    at = (s % SETS_PER_SINE) * SETS_PER_SINE * L
                    act.activation(sins[:, m % SINS, at:at + SETS_PER_SINE * L].rearrange("p (t l) -> p t l", l=L),
                                   ps[:, (s % SETS) * SETS_PER_SINE:(s % SETS + 1) * SETS_PER_SINE, :],
                                   ACT.Sin, scale=-TWO_PI_DOWN).then_inc(b_sin, 1)

            def sigmoids(b, half):
                for u in range(UNITS):
                    h = half * UNITS + u
                    act.wait_ge(b_fma, b * ADDS_ROW + half * ADDS_HALF + last_addition(u) + SINE_CREDIT)
                    act.activation(acc[:, u, :], acc[:, u, :], ACT.Sigmoid,
                                   scale=alpha_s[:, h, NF - 1:NF]).then_inc(b_sig, 1)

            def row(b, last):
                for half in range(HALVES):
                    sines(b, half)
                    sigmoids(b, half)
            with act.Fori(0, B - 1) as b:
                row(b, False)
            row(B - 1, True)

            pipelined(act, ((3, normalise(hTo, lambda j: by_token(C_Y(j)), 2, c_yn)),
                            (4, normalise(xn, lambda j: yv[j], 3, c_n)),
                            (5, tanh(C_FF, c_ff, c_th, c_st)),
                            (4, copy_transposed(xnT, C_TR, c_t, c_c))))

        @block.vector
        def _(dve):
            dve.wait_ge(s_const, N_CONST * 16)
            steps = [0]

            def then_wait(ins):
                steps[0] += 1
                ins.then_inc(s_tab_step, 1)
                dve.wait_ge(s_tab_step, steps[0])

            then_wait(nc.vector.tensor_scalar(phit[:, :, :], phi4[:, :, :], float(1 / (2 * np.pi)), None, ALU.mult))
            dve.wait_ge(s_wps, 2)
            nc.vector.tensor_copy(wq_s[:, :, :], ps[:, 1:1 + NQ, 0:P])
            nc.vector.tensor_copy(wk_s[:, :, :], ps[:, 1:1 + NQ, P:2 * P])
            dve.wait_ge(s_wps, 3)
            nc.vector.tensor_copy(gb_bc[:, :, :], ps[:, 5, P:3 * P].rearrange("p (a n) -> p a n", a=2))
            nc.vector.tensor_copy(bv_bc[:, :], ps[:, 5, 3 * P:4 * P])
            then_wait(nc.vector.tensor_copy(alpha_bc[:, :], ps[:, 5, 0:H * NF + 1]))
            al = alpha_bc[:, 0:H * NF].rearrange("p (h f) -> p h f", h=H)
            then_wait(nc.vector.tensor_scalar(a_neg[:, :, :], al, 0.0, None, ALU.is_lt))
            then_wait(nc.vector.tensor_scalar(a_neg[:, :, :], a_neg[:, :, :], -2.0, 1.0, ALU.mult, ALU.add))
            then_wait(nc.vector.tensor_tensor(a_abs[:, :, :], al, a_neg[:, :, :], ALU.mult))
            then_wait(nc.vector.tensor_scalar(a_abs[:, :, :], a_abs[:, :, :], TINY, None, ALU.max))
            then_wait(nc.vector.tensor_tensor(alpha_s[:, :, :], a_abs[:, :, :], a_neg[:, :, :], ALU.mult))
            then_wait(nc.vector.reciprocal(a_neg[:, :, :], alpha_s[:, :, :]))
            then_wait(nc.vector.tensor_tensor(ratio[:, :, :], alpha_s[:, :, 0:NF - 1], a_neg[:, :, 1:NF], ALU.mult))
            temp = alpha_bc[:, H * NF:]
            then_wait(nc.vector.scalar_tensor_tensor(out=itemp[:, 0:1], in0=temp, scalar=-1.0, in1=temp,
                                                     op0=ALU.mult, op1=ALU.max))
            then_wait(nc.vector.tensor_scalar(itemp[:, 1:2], itemp[:, 0:1], 0.1, None, ALU.add))
            then_wait(nc.vector.reciprocal(itemp[:, 2:3], itemp[:, 1:2]))
            for f, freq in enumerate(FREQS):
                last = nc.vector.tensor_scalar(s_f[:, f:f + 1], itemp[:, 2:3], float(1 / (np.sqrt(HD) * freq)), None, ALU.mult)
            then_wait(last)
            then_wait(nc.vector.tensor_scalar(s_f[:, :], s_f[:, :], cst[:, C_QROW:C_QROW + 1], cst[:, C_MROW:C_MROW + 1],
                                              ALU.mult, ALU.add))
            dve.wait_ge(s_wps, 4)
            nc.vector.tensor_scalar(bq_c[:, :], ps[:, 6, 0:NQ], cst[:, C_ONE:C_ONE + 1], None, ALU.add)
            nc.vector.tensor_scalar(bk_c[:, :], ps[:, 6, NQ:2 * NQ], cst[:, C_ONE:C_ONE + 1], None, ALU.add)
            for q in range(NQ):
                last = nc.vector.tensor_tensor(s_tab[:, q, :], ps[:, 6, P + NF * q:P + NF * (q + 1)], s_f[:, :], ALU.add)
            then_wait(last)
            nc.vector.tensor_scalar(gs[:, :, :], s_tab[:, :, :], cst[:, C_QG:C_QG + 1], None, ALU.mult)
            then_wait(nc.vector.tensor_scalar(bs[:, :, :], s_tab[:, :, :], cst[:, C_QB:C_QB + 1], None, ALU.mult))
            dve.wait_ge(s_wsb, 5)
            dve.wait_ge(s_ones, 5)
            nc.vector.tensor_copy(itemp[:, 0:1], itemp[:, 1:2]).then_inc(s_setup, 1)

            def moments(src, k, ready=None):
                def work(row, turn, j):
                    if ready:
                        dve.wait_ge(ready, row + 1)
                    for t in range(TC):
                        last = nc.vector.bn_stats(out=stats[:, j, k % 2, t, :], in_=src(j)[:, t, :])
                    last.then_inc(m_stats[k], 1)
                    dve.wait_ge(m_stats[k], row + 1)
                    alone(dve, "vector")
                    for t in range(TC):
                        last = nc.vector.bn_aggr(out=mv[:, j, k % 2, t, :], in_=stats[:, j, k % 2, t, :])
                    last.then_inc(m_mv[k], 1)
                    dve.wait_ge(m_mv[k], row + 1)
                    nc.vector.tensor_scalar(nmean[:, j, k % 2, :], mv[:, j, k % 2, :, 0], -1.0, None, ALU.mult)
                    nc.vector.tensor_scalar(vare[:, j, k % 2, :], mv[:, j, k % 2, :, 1], EPS, None, ALU.add).then_inc(m_var[k], 1)
                return work

            def x_moments(row, turn, j):
                dve.wait_ge(a_x[j], (turn + 1) * 16)
                moments(lambda j: xin[j], 0)(row, turn, j)

            def make_x1(row, turn, j):
                dve.wait_ge(a_stx[j], turn * 16 + DMA_CREDIT)
                dve.wait_ge(a_th, row + 1)
                nc.vector.scalar_tensor_tensor(out=x1t[j], in0=th[j], scalar=0.5, in1=xin[j],
                                               op0=ALU.mult, op1=ALU.add).then_inc(a_x1, 1)
                dve.wait_ge(a_x1, row + 1 + ROW_CREDIT)
                moments(lambda j: x1t[j], 1)(row, turn, j)

            pipelined(dve, ((3, make_x1), (0, x_moments)))

            dve.sem_inc(b_fma, SINE_CREDIT)
            STEPS_QUAD = 2 * NF

            def split(b, q):
                n = b * NQ + q
                first = isinstance(n, int) and n == 0
                slot = q % QPH
                k_bank, q_bank = KQ_BANKS[slot]
                k_pos, k_neg = ks[:, slot, 0, :], ks[:, slot, 1, :]

                def stepped(k):
                    dve.wait_ge(b_step, n * STEPS_QUAD + k)

                def high(f):
                    nc.vector.tensor_scalar(hi_r[:, (f + 1) % 3, :], xq[:, :], gs[:, q, f:f + 1], None, ALU.mult).then_inc(b_step, 1)

                def side(f):
                    return nc.vector.scalar_tensor_tensor(out=q_r[:, slot, f, :], in0=xq[:, :], scalar=bs[:, q, f:f + 1],
                                                          in1=hi_r[:, (f + 1) % 3, :].bitcast(F32),
                                                          op0=ALU.mult, op1=ALU.subtract)

                dve.wait_ge(b_kps, n + 1)
                nc.vector.tensor_scalar(xk[:, :], ps[:, k_bank, :], bk_c[:, q:q + 1], None, ALU.add).then_inc(b_xk, 1)
                if not first:
                    dve.wait_ge(b_qr, n)
                dve.wait_ge(b_qps, n + 1)
                nc.vector.tensor_scalar(xq[:, :], ps[:, q_bank, :], bq_c[:, q:q + 1], None, ALU.add).then_inc(b_xq, 1)
                dve.wait_ge(b_xk, n + 1)
                nc.vector.tensor_scalar(hi_r[:, 0, :], xk[:, :], cst[:, C_KG:C_KG + 1], None, ALU.mult).then_inc(b_step, 1)
                dve.wait_ge(b_xq, n + 1)
                high(0)
                stepped(1)
                nc.vector.scalar_tensor_tensor(out=k_pos, in0=xk[:, :], scalar=cst[:, C_KB:C_KB + 1],
                                               in1=hi_r[:, 0, :].bitcast(F32), op0=ALU.mult, op1=ALU.subtract).then_inc(b_kp, 1)
                high(1)
                dve.wait_ge(b_kp, n + 1)
                nc.vector.tensor_scalar(k_neg, k_pos.bitcast(F32), cst[:, C_KNEG:C_KNEG + 1], None, ALU.mult).then_inc(b_ks, 1)
                for f in range(NF):
                    stepped(f + 2 if f < 2 else 2 * f + 1)
                    if f + 1 == NF:
                        side(f).then_inc(b_qr, 1)
                    else:
                        side(f).then_inc(b_step, 1)
                    if f + 2 < NF:
                        if f > 0:
                            stepped(2 + 2 * f)
                        high(f + 2)

            def copy_values(b):
                dve.wait_ge(b_vps, b + 1)
                nc.vector.tensor_tensor(v_s[:, :, :, 0:HD], ps[:, BK_A, :].rearrange("p (t h d) -> p t h d", t=TC, h=H),
                                        bv_bc[:, :].rearrange("p (o h d) -> p o h d", o=1, h=H).to_broadcast([P, TC, H, HD]),
                                        ALU.add).then_inc(b_v, 1)

            def add_sines(b, half):
                base = b * ADDS_ROW + half * ADDS_HALF + SINE_CREDIT
                for m, (unit, f) in enumerate(order(half)):
                    q = half * QPH + unit // G
                    h = q * G + unit % G
                    dve.wait_ge(b_sin, b * SETS_ROW + half * SETS_HALF + SETS_PER_SINE * (m + 1) + SET_CREDIT)
                    if f == 0:
                        continue
                    if f == 1:
                        dve.wait_ge(b_pv, b * NQ + q - QPH + 1 + PV_CREDIT)
                        before = sins[:, (m - 2) % SINS, :]
                    else:
                        dve.wait_ge(b_fma, base + added(m) - 2)
                        before = acc[:, unit, :]
                    ins = nc.vector.scalar_tensor_tensor(out=acc[:, unit, :], in0=before, scalar=ratio[:, h, f - 1:f],
                                                         in1=sins[:, m % SINS, :], op0=ALU.mult, op1=ALU.add)
                    ins.then_inc(b_fma, 1)

            def copy_pv(b, half, q):
                slot = q % QPH
                dve.wait_ge(b_st[slot], (b * HALVES + half) * STORES * 16 + STORE_CREDIT)
                dve.wait_ge(b_pv, b * NQ + q + 1 + PV_CREDIT)
                nc.vector.tensor_copy(o_sb[:, slot, :], ps[:, (BK_A, BK_B)[slot], :]).then_inc(b_o, 1)

            dve.sem_inc(b_o, COPY_CREDIT)
            for q in range(QPH):
                split(0, q)
            copy_values(0)

            def row(b, last):
                for half in range(HALVES):
                    end = half == 1 and last
                    add_sines(b, half)
                    nb, nh = (b, 1) if half == 0 else (b + 1, 0)
                    if not end:
                        for q in range(QPH * nh, QPH * (nh + 1)):
                            split(nb, q)
                    for q in range(QPH * half, QPH * (half + 1)):
                        copy_pv(b, half, q)
                    if half == 1 and not end:
                        copy_values(b + 1)
            with dve.Fori(0, B - 1) as b:
                row(b, False)
            row(B - 1, True)

            dve.wait_ge(c_den, 16)
            nc.vector.tensor_scalar(den_a, den_a, 1e-10, None, ALU.add).then_inc(c_eps, 1)
            dve.wait_ge(c_eps, 1)
            nc.vector.reciprocal(den_a, den_a).then_inc(c_rden, 1)

            def normalise_heads(row, turn, j):
                dve.wait_ge(c_sp, row + 1)
                nc.vector.tensor_tensor(xin[j], xin[j], by_token(C_SP(j)), ALU.mult).then_inc(c_on, 1)

            def add_attention(row, turn, j):
                dve.wait_ge(c_yn, row + 1)
                nc.vector.tensor_tensor(hTo[j], hTo[j], gb_bc[:, 0:1, :].to_broadcast([P, TC, D]), ALU.mult).then_inc(c_yg, 1)
                dve.wait_ge(c_xb, row + 1 + ROW_CREDIT)
                dve.wait_ge(c_yg, row + 1)
                nc.vector.tensor_tensor(yv[j], hTo[j], hn[j], ALU.add).then_inc(c_x2, 1)

            def make_out(row, turn, j):
                dve.wait_ge(c_th, row + 1)
                nc.vector.scalar_tensor_tensor(out=th[j], in0=th[j], scalar=0.5, in1=yv[j],
                                               op0=ALU.mult, op1=ALU.add).then_inc(c_out, 1)

            def y_moments(row, turn, j):
                dve.wait_ge(c_y, row + 1 + ROW_CREDIT)
                moments(lambda j: by_token(C_Y(j)), 2)(row, turn, j)

            pipelined(dve, ((1, normalise_heads), (6, make_out), (2, y_moments), (3, add_attention),
                            (3, moments(lambda j: yv[j], 3, c_x2))))


NAMES = ['L0_attn_x', 'L0_attn_Wq', 'L0_attn_bq', 'L0_attn_Wk', 'L0_attn_bk', 'L0_attn_Wv', 'L0_attn_bv',
         'L0_attn_Wo', 'L0_attn_bo', 'L0_attn_alpha', 'L0_attn_phi', 'L0_attn_temperature', 'L0_attn_gamma',
         'L0_attn_beta', 'L0_ffn_weight', 'L0_ffn_aux_weight1', 'L0_ffn_aux_weight2', 'L0_ffn_bias']


def kernel(**inputs):
    import concourse.bacc as bacc
    from concourse.bass_utils import run_bass_kernel_spmd

    nc = bacc.Bacc("TRN2", target_bir_lowering=False, num_devices=1)
    arrays, args = {}, []
    for name in NAMES:
        a = np.ascontiguousarray(inputs[name])
        arrays[f"in_{name}"] = a
        args.append(nc.dram_tensor(f"in_{name}", a.shape, mybir.dt.from_np(a.dtype), kind="ExternalInput").ap())
    c = constants()
    arrays["in_consts"] = c
    args.append(nc.dram_tensor("in_consts", c.shape, mybir.dt.float32, kind="ExternalInput").ap())
    args.append(nc.dram_tensor("out", (B, L, D), mybir.dt.float32, kind="ExternalOutput").ap())
    build(nc, *args)
    r = run_bass_kernel_spmd(nc, [arrays], core_ids=[0])
    return r.results[0]["out"]
```

```python
import numpy as np
import concourse.bass as bass
from concourse import mybir
from contextlib import ExitStack

B, L, D = 16, 512, 128
H, HD = 16, 8
FREQS = (31.0, 37.0, 41.0, 43.0, 47.0)
NF = len(FREQS)
P = 128
TC = L // P
G = 4
NQ = H // G
R = P // G
HALVES = 2
QPH = NQ // HALVES
UNITS = QPH * G
SINS = 5
SETS = 3
SETS_PER_SINE = 2
MAGIC = 1.5 * 2.0 ** 23
TWO_PI_DOWN = float(np.nextafter(np.float32(2 * np.pi), np.float32(0)))
EPS = 1e-5
TINY = 1e-18

C_IDENT, C_REP, C_PHIREP = 0, 128, 256
C_QG, C_QB, C_KG, C_KB, C_KNEG, C_MROW, C_QROW, C_ONE, C_BG, C_BB = range(384, 394)
NCONST = 394


def constants():
    c = np.zeros((P, NCONST), np.float32)
    c[:, C_IDENT:C_IDENT + P] = np.eye(P)
    r = np.arange(P) % R
    for k in range(P):
        head, d = (k % R) // HD, k % HD
        for part in range(3):
            c[k, C_REP + R * head + HD * part + d] = 1.0
    for k in range(G):
        c[k, C_PHIREP + R * k + 24:C_PHIREP + R * k + 26] = 1.0
    q_low = (r < 8) | (r == 25)
    k_low = (r >= 8) & (r < 16)
    c[:, C_QG], c[:, C_QB] = np.where(q_low, 1, -1), np.where(q_low, 1, 0)
    c[:, C_KG], c[:, C_KB] = np.where(k_low, 1, -1), np.where(k_low, 1, 0)
    c[0:2, C_BG], c[0:2, C_BB] = (-1, 1), (0, 1)
    c[:, C_KNEG] = -1.0 * (r < 26)
    c[:, C_MROW] = np.where(r == 26, MAGIC, np.where(r == 27, -MAGIC, 0))
    c[:, C_QROW] = r < 24
    c[:, C_ONE] = (r >= 24) & (r < 28)
    return c


def build(nc, x, Wq, bq, Wk, bk, Wv, bv, Wo, bo, alpha, phi, temperature, gamma, beta,
          W1, W2, W3, bias, consts, out):
    F32, F32R = mybir.dt.float32, mybir.dt.float32r
    ALU, ACT = mybir.AluOpType, mybir.ActivationFunctionType
    ctx = ExitStack()
    with ctx:
        def sb(name, shape, dt=F32):
            return ctx.enter_context(nc.sbuf_tensor(name, shape, dt))

        def sem(name):
            return ctx.enter_context(nc.semaphore(name))

        x1_d = nc.dram_tensor("x1_scratch", (B, P, TC, D), F32).ap()
        hT_d = nc.dram_tensor("hT_scratch", (B, D, L), F32).ap()
        oT_d = nc.dram_tensor("oT_scratch", (B, D, L), F32).ap()
        den_d = nc.dram_tensor("den_scratch", (B + 1, H, L), F32).ap()
        rden_d = nc.dram_tensor("rden_scratch", (B + 1, H, L), F32).ap()

        cst = sb("cst", [P, NCONST])
        ident = cst[:, C_IDENT:C_IDENT + P]
        wq_s = sb("wq_s", [P, NQ, P])
        wk_s = sb("wk_s", [P, NQ, P])
        wvT = sb("wvT", [P, P])
        woT = sb("woT", [P, P])
        w1T = sb("w1T", [P, P])
        w12T = sb("w12T", [P, P])
        wf = sb("wf", [P, P])
        rows = sb("rows", [1, 3, P])
        bias2 = sb("bias2", [2, 2, P])
        bias_hi = sb("bias_hi", [2, 2, P], F32R)
        bias_r = sb("bias_r", [2, 2, P], F32R)
        ones_r = sb("ones_r", [2, P], F32R)
        misc = sb("misc", [1, H * NF + 1])
        bqk = sb("bqk", [R, 2, NQ])
        phi4 = sb("phi4", [G, NQ, NF])
        phit = sb("phit", [G, NQ, NF])
        ones = sb("ones", [P, P])
        alpha_bc = sb("alpha_bc", [P, H * NF + 1])
        a_neg = sb("a_neg", [P, H, NF])
        a_abs = sb("a_abs", [P, H, NF])
        alpha_s = sb("alpha_s", [P, H, NF])
        ratio = sb("ratio", [P, H, NF - 1])
        gb_bc = sb("gb_bc", [P, 2, P])
        bq_c = sb("bq_c", [P, NQ])
        bk_c = sb("bk_c", [P, NQ])
        itemp = sb("itemp", [P, 3])
        s_f = sb("s_f", [P, NF])
        s_tab = sb("s_tab", [P, NQ, NF])
        gs = sb("gs", [P, NQ, NF])
        bs = sb("bs", [P, NQ, NF])
        mhalf = sb("mhalf", [P, TC])

        sins = sb("sins", [P, SINS, TC * L])
        acc = sb("acc", [P, UNITS, TC * L])
        q_r = sb("q_r", [P, QPH, NF, L], F32R)
        k_r = sb("k_r", [P, QPH, 2, G, L], F32R)
        hi_r = sb("hi_r", [P, 3, L], F32R)
        xq = sb("xq", [P, QPH, L])
        xk = sb("xk", [P, L])
        ks = sb("ks", [P, QPH, 2, L], F32R)
        v_s = sb("v_s", [P, TC, H, R])
        bv_bc = sb("bv_bc", [P, P])
        hT = sb("hT", [P, L])
        o_sb = sb("o_sb", [P, QPH, L])
        den_row = sb("den_row", [P, H * L // P])
        wnat = sins[:, 0, 0:7 * P].rearrange("p (w n) -> p w n", w=7)

        NS = 4

        def tile(k):
            return [acc[:, k, L * j:L * (j + 1)].rearrange("p (t d) -> p t d", t=TC) for j in range(NS)]

        xin, xn, xnT, th, x1t, hn, hTo, yv = (tile(k) for k in range(UNITS))
        rdc = [sins[:, 1, L * j:L * (j + 1)] for j in range(NS)]
        small_at = [0]

        def small(*shape):
            n, at = int(np.prod(shape)), small_at[0]
            small_at[0] += n
            names = "abcd"[:len(shape)]
            return sins[:, SINS - 1, at:at + n].rearrange(f"p ({' '.join(names)}) -> p {' '.join(names)}",
                                                          **dict(zip(names, shape)))

        stats = small(NS, 2, TC, 6)
        mv = small(NS, 2, TC, 2)
        vare = small(NS, 2, TC)
        nmean = small(NS, 2, TC)
        rstd = small(NS, 2, TC)
        nmr = small(NS, 2, TC)

        ps = ctx.enter_context(nc.psum_tensor("ps", [P, 8, L], F32))
        BK_A, BK_B = 6, 7
        V_BANK = 0
        VH = D // HALVES
        KQ_BANKS = ((BK_A, BK_B), (2 * SETS - 2, 2 * SETS - 1))

        s_w = sem("weights_loaded")
        s_const = sem("consts_loaded")
        s_phi = sem("phases_in_turns")
        s_tables = sem("tables_ready")
        s_ones = sem("ones_set")
        s_wps = sem("setup_product_ready")
        s_wsb = sem("setup_product_copied")
        s_tab_step = sem("setup_table_step")
        s_setup = sem("setup_done")
        m_stats = [sem(f"ac_stats_{k}") for k in range(4)]
        m_mv = [sem(f"ac_mean_and_variance_{k}") for k in range(4)]
        m_var = [sem(f"ac_guarded_variance_{k}") for k in range(4)]
        m_rstd = [sem(f"ac_rstd_{k}") for k in range(4)]
        m_nmr = [sem(f"ac_shift_{k}") for k in range(4)]
        a_x = [sem(f"a_x_loaded_{j}") for j in range(NS)]
        a_n1 = sem("a_x_normalised")
        a_t1 = sem("a_x_transposed_in_psum")
        a_c1 = sem("a_x_transposed_in_sbuf")
        a_ff = sem("a_ffn_in_psum")
        a_th = sem("a_tanh_ready")
        a_x1 = sem("a_x1_ready")
        a_n2 = sem("a_x1_normalised")
        a_t2 = sem("a_x1_transposed_in_psum")
        a_c2 = sem("a_x1_transposed_in_sbuf")
        a_stx = [sem(f"a_x1_stored_{j}") for j in range(NS)]
        a_sth = [sem(f"a_hT_stored_{j}") for j in range(NS)]
        b_h = sem("b_hT_loaded")
        b_kps = sem("b_k_in_psum")
        b_qps = sem("b_q_in_psum")
        b_vps = sem("b_v_in_psum")
        b_xk = sem("b_k_biased")
        b_xq = sem("b_q_biased")
        b_v = sem("b_v_copied")
        b_step = sem("b_vector_split_step")
        b_kp = sem("b_k_split")
        b_ks = sem("b_k_negated")
        b_kr = [[sem(f"b_k_side_ready_{slot}_{g}") for g in range(G)] for slot in range(QPH)]
        b_qr = sem("b_q_sides_ready")
        b_t = sem("b_angles_ready")
        b_sin = sem("b_sines_ready")
        b_fma = sem("b_sine_added")
        b_sig = sem("b_sigmoids_ready")
        b_pv = sem("b_pv_in_psum")
        b_o = sem("b_pv_copied")
        b_st = [sem(f"b_heads_stored_{slot}") for slot in range(QPH)]
        b_den = sem("b_denominators_loaded")
        b_eps = sem("b_denominators_guarded")
        b_rden = sem("b_reciprocals_ready")
        b_rst = sem("b_reciprocals_stored")
        c_lo = [sem(f"c_heads_loaded_{j}") for j in range(NS)]
        c_lx = [sem(f"c_x1_loaded_{j}") for j in range(NS)]
        c_on = sem("c_heads_normalised")
        c_y = sem("c_projection_in_psum")
        c_xb = sem("c_beta_added")
        c_yn = sem("c_projection_normalised")
        c_yg = sem("c_times_gamma")
        c_x2 = sem("c_attention_added")
        c_n = sem("c_x2_normalised")
        c_t = sem("c_x2_transposed_in_psum")
        c_c = sem("c_x2_transposed_in_sbuf")
        c_ff = sem("c_ffn_in_psum")
        c_th = sem("c_tanh_ready")
        c_out = sem("c_out_ready")
        c_st = [sem(f"c_out_stored_{j}") for j in range(NS)]

        N_WEIGHTS, N_CONST = 12, 8

        s_passed = {name: sem(f"waits_passed_by_{name}") for name in ("sync", "pool", "vector")}

        def alone(eng, name):
            eng.sem_inc(s_passed[name], 1)

        ROW_CREDIT, DMA_CREDIT = NS, 16

        def by_token(bank):
            return ps[:, bank, :].rearrange("p (t d) -> p t d", t=TC)

        def A_TR(j): return 1 + j % 2
        def A_FF(j): return 3
        def C_Y(j): return j
        def C_TR(j): return 4 + j % 2
        def C_FF(j): return 6 + j % 2

        def pipelined(eng, stages):
            peeled = max(1, -(-max(lag for lag, _ in stages) // NS))
            for step in range(peeled * NS):
                for lag, work in stages:
                    if step >= lag:
                        work(step - lag, (step - lag) // NS, (step - lag) % NS)
            with eng.Fori(peeled, B // NS) as i:
                for j in range(NS):
                    for lag, work in stages:
                        work(i * NS + (j - lag), i + (j - lag) // NS, (j - lag) % NS)
            for step in range(B, B + max(lag for lag, _ in stages)):
                for lag, work in stages:
                    if step - lag < B:
                        work(step - lag, (step - lag) // NS, (step - lag) % NS)

        block = ctx.enter_context(nc.Block())

        SETS_HALF = UNITS * NF * SETS_PER_SINE
        SETS_ROW = HALVES * SETS_HALF
        SINES_HALF = UNITS * NF
        UNITS_ROW = HALVES * UNITS
        SET_CREDIT, SINE_CREDIT, PV_CREDIT, COPY_CREDIT = SETS, SINS, QPH, 1
        STORES = G + 1
        STORE_CREDIT = 16

        def order():
            return [(2 * pair + a, f) for pair in range(UNITS // 2) for f in range(NF) for a in range(2)]

        ADDS_HALF = UNITS * (NF - 1)
        ADDS_ROW = HALVES * ADDS_HALF

        def added(m):
            return len([f for _, f in order()[:m + 1] if f > 0])

        def last_addition(unit):
            return added(max(m for m, (u, f) in enumerate(order()) if u == unit))

        def freed(m):
            return added(m + 2 if order()[m][1] == 0 else m)

        @block.sync
        def _(sp):
            sp.dma_start(cst[:, :], consts).then_inc(s_w, 16)
            for n, w in enumerate((Wq, Wk, Wv, Wo, W1, W2, W3)):
                sp.dma_start(wnat[:, n, :], w).then_inc(s_w, 16)
            for n, v in enumerate((bo, bias)):
                for part in range(2):
                    sp.dma_start(bias2[part:part + 1, n, :], v.rearrange("(a n) -> a n", a=1)).then_inc(s_w, 16)
            for j in range(NS):
                sp.sem_inc(a_stx[j], DMA_CREDIT)
                sp.sem_inc(a_sth[j], DMA_CREDIT)
            sp.sem_inc(a_x1, ROW_CREDIT)

            def load_rest(row, turn, j):
                if not (isinstance(row, int) and row == 1):
                    return
                for n, v in enumerate((bv, gamma, beta)):
                    sp.dma_start(rows[0:1, n, :], v.rearrange("(a n) -> a n", a=1)).then_inc(s_const, 16)
                sp.dma_start(misc[0:1, 0:H * NF], alpha.rearrange("(a h) f -> a (h f)", a=1)).then_inc(s_const, 16)
                sp.dma_start(misc[0:1, H * NF:], temperature.rearrange("(a n) -> a n", a=1)).then_inc(s_const, 16)
                sp.dma_start(phi4[:, :, :], phi.rearrange("(q g) f -> g q f", g=G)).then_inc(s_const, 16)

                sp.dma_start(bqk[:, 0, :], bq.rearrange("(q p) -> p q", p=R), allow_slow_non_contiguous=True).then_inc(s_const, 16)
                sp.dma_start(bqk[:, 1, :], bk.rearrange("(q p) -> p q", p=R), allow_slow_non_contiguous=True).then_inc(s_const, 16)

            def load_x(row, turn, j):
                sp.wait_ge(a_x1, row + 1)
                alone(sp, "sync")
                sp.dma_start(xin[j], x[bass.ds(row, 1)].rearrange("o (p t) d -> p (o t) d", t=TC)).then_inc(a_x[j], 16)

            def store_x1(row, turn, j):
                sp.wait_ge(a_x1, row + 1 + ROW_CREDIT)
                alone(sp, "sync")
                sp.dma_start(x1_d[bass.ds(row, 1)].rearrange("o p t d -> p (o t) d"), x1t[j]).then_inc(a_stx[j], 16)

            def store_hT(row, turn, j):
                sp.wait_ge(a_c2, row + 1)
                alone(sp, "sync")
                sp.dma_start(hT_d[bass.ds(row, 1)].rearrange("o d l -> d (o l)"),
                             hTo[j].rearrange("p t d -> p (t d)")).then_inc(a_sth[j], 16)

            def first_hT(row, turn, j):
                if isinstance(row, int) and row == B - NS:
                    sp.wait_ge(a_sth[0], (B // NS - 1) * 16 + DMA_CREDIT)
                    sp.dma_start(hT[:, :], hT_d[0]).then_inc(b_h, 16)

            pipelined(sp, ((0, load_x), (0, load_rest), (4, store_x1), (4, first_hT), (6, store_hT)))

            for slot in range(QPH):
                sp.sem_inc(b_st[slot], STORE_CREDIT)

            def k_sides(i, q):
                sp.wait_ge(b_ks, i * NQ + q + 1)
                alone(sp, "sync")
                for g in range(G):
                    rows_g = slice(R * g, R * (g + 1))
                    sp.dma_start(k_r[rows_g, q % QPH, :, g, :].bitcast(F32), ks[rows_g, q % QPH, :, :].bitcast(F32)).then_inc(b_kr[q % QPH][g], 16)

            def store_heads(i, q):
                sp.wait_ge(b_o, i * NQ + q + 1 + COPY_CREDIT)
                alone(sp, "sync")
                for g in range(G):
                    sp.dma_start(oT_d[bass.ds(i, 1), (q * G + g) * HD:(q * G + g + 1) * HD, :].rearrange("o d l -> d (o l)"),
                                 o_sb[R * g:R * g + HD, q % QPH, :]).then_inc(b_st[q % QPH], 16)
                sp.dma_start(den_d[bass.ds(i + 1, 1), q * G:(q + 1) * G, :].rearrange("o h l -> h (o l)"),
                             o_sb[HD:HD + R * (G - 1) + 1:R, q % QPH, :]).then_inc(b_st[q % QPH], 16)

            def spread_row(d, i):
                return d[bass.ds(i, 1)].rearrange("o h (s l) -> (o h s) l", s=P // H)

            def load_denominators(i):
                for slot in range(QPH):
                    sp.wait_ge(b_st[slot], i * HALVES * STORES * 16 + STORE_CREDIT)
                    alone(sp, "sync")
                sp.wait_ge(b_rst, (i + 1) * 16)
                alone(sp, "sync")
                sp.dma_start(den_row[:, :], spread_row(den_d, i)).then_inc(b_den, 16)

            def store_reciprocals(i):
                sp.wait_ge(b_rden, i + 1)
                alone(sp, "sync")
                sp.dma_start(spread_row(rden_d, i), den_row[:, :]).then_inc(b_rst, 16)

            def row(i, last):
                for half in range(HALVES):
                    ni, nh = (i, 1) if half == 0 else (i + 1, 0)
                    if not (half == 1 and last):
                        for q in range(QPH * nh, QPH * (nh + 1)):
                            k_sides(ni, q)
                    if half == 0 and not last:
                        sp.wait_ge(b_qps, i * NQ + NQ)
                        alone(sp, "sync")
                        sp.dma_start(hT[:, :], hT_d[bass.ds(i + 1, 1)].rearrange("o d l -> d (o l)")).then_inc(b_h, 16)
                    if half == 0:
                        load_denominators(i)
                    for q in range(QPH * half, QPH * (half + 1)):
                        store_heads(i, q)
                    if half == 0:
                        store_reciprocals(i)
            sp.wait_ge(s_ones, 5)
            sp.dma_start(spread_row(den_d, 0), ones[:, 0:H * L // P]).then_inc(b_rst, 16)
            for q in range(QPH):
                k_sides(0, q)
            for j in range(NS):
                sp.wait_ge(a_stx[j], B // NS * 16 + DMA_CREDIT)
                sp.wait_ge(a_sth[j], B // NS * 16 + DMA_CREDIT)
            with sp.Fori(0, B - 1) as i:
                row(i, False)
            row(B - 1, True)
            load_denominators(B)

            for j in range(NS):
                sp.sem_inc(c_st[j], DMA_CREDIT)
            sp.sem_inc(c_y, ROW_CREDIT)
            sp.sem_inc(c_xb, ROW_CREDIT)

            def load_heads(row, turn, j):
                sp.wait_ge(c_y, row + 1)
                alone(sp, "sync")
                sp.dma_start(xin[j].rearrange("p t d -> p (t d)"),
                             oT_d[bass.ds(row, 1)].rearrange("o d l -> d (o l)")).then_inc(c_lo[j], 16)
                sp.dma_start(rdc[j], rden_d[bass.ds(row + 1, 1)].rearrange("o (h d) l -> (o h) d l", d=1)
                             .to_broadcast([H, HD, L])).then_inc(c_lo[j], 16)

            def load_x1(row, turn, j):
                sp.wait_ge(c_xb, row + 1)
                alone(sp, "sync")
                sp.dma_start(x1t[j], x1_d[bass.ds(row, 1)].rearrange("o p t d -> p (o t) d")).then_inc(c_lx[j], 16)

            def store_out(row, turn, j):
                sp.wait_ge(c_out, row + 1)
                alone(sp, "sync")
                sp.dma_start(out[bass.ds(row, 1)].rearrange("o (p t) d -> p (o t) d", t=TC), th[j]).then_inc(c_st[j], 16)

            def last_reciprocals(row, turn, j):
                if isinstance(row, int) and row == NS - 1:
                    store_reciprocals(B)
                    sp.wait_ge(b_rst, (B + 2) * 16)

            pipelined(sp, ((0, load_heads), (1, load_x1), (0, last_reciprocals), (8, store_out)))
            for j in range(NS):
                sp.wait_ge(c_st[j], B // NS * 16 + DMA_CREDIT)

        @block.tensor
        def _(pe):
            pe.wait_ge(s_w, N_WEIGHTS * 16)
            pe.wait_ge(s_ones, 1)
            one = ones[0:1, 0:P]
            nc.tensor.transpose(ps[:, 0, 0:P], wnat[:, 2, :], ident)
            nc.tensor.transpose(ps[:, 0, P:2 * P], wnat[:, 3, :], ident)
            nc.tensor.transpose(ps[:, 0, 2 * P:3 * P], wnat[:, 4, :], ident).then_inc(s_wps, 1)
            for q in range(NQ):
                rep = slice(R * q, R * (q + 1))
                for n in range(2):
                    mm = nc.tensor.matmul(ps[:, 1 + q, P * n:P * (n + 1)], wnat[rep, n, :],
                                          cst[rep, C_REP:C_REP + P], start=True, stop=True)
            mm.then_inc(s_wps, 1)
            pe.wait_ge(s_wsb, 3)
            nc.tensor.matmul(ps[:, 7, 0:P], wnat[:, 5, :], w1T[:, :], start=True, stop=True).then_inc(s_wps, 1)
            pe.wait_ge(s_wsb, 4)
            nc.tensor.matmul(ps[:, 7, P:2 * P], w12T[:, :], wnat[:, 6, :], start=True, stop=True).then_inc(s_wps, 1)
            pe.wait_ge(s_wsb, 5)
            pe.wait_ge(s_setup, 1)

            def spread_tables(row, turn, j):
                if not (isinstance(row, int) and row == 0):
                    return
                pe.wait_ge(s_const, N_CONST * 16)
                nc.tensor.matmul(ps[:, 5, 0:H * NF + 1], one, misc[0:1, :], start=True, stop=True)
                nc.tensor.matmul(ps[:, 5, P:P + 2 * P], one, rows[0:1, 1:3, :], start=True, stop=True)
                nc.tensor.matmul(ps[:, 5, 3 * P:4 * P], one, rows[0:1, 0, :], start=True, stop=True).then_inc(s_wps, 1)
                nc.tensor.matmul(ps[:, 6, 0:2 * NQ], cst[0:R, C_REP:C_REP + P], bqk[:, :, :], start=True, stop=True)
                pe.wait_ge(s_phi, 1)
                nc.tensor.matmul(ps[:, 6, P:P + NQ * NF], cst[0:G, C_PHIREP:C_PHIREP + P], phit[:, :, :],
                                 start=True, stop=True).then_inc(s_wps, 1)

            def transposes(src, bank, ready, done):
                def work(row, turn, j):
                    pe.wait_ge(ready, row + 1)
                    for t in range(TC):
                        mm = nc.tensor.transpose(ps[:, bank(j), P * t:P * (t + 1)], src[j][:, t, :], ident)
                    mm.then_inc(done, 1)
                return work

            def fill_bias(bank, n):
                nc.tensor.matmul(ps[:, bank, :], ones_r[:, :], bias_r[:, n:n + 1, :].to_broadcast([2, TC, P]),
                                 start=True, stop=False)

            def feed_forward(bank, ready, done):
                def work(row, turn, j):
                    pe.wait_ge(ready, row + 1)
                    fill_bias(bank(j), 1)
                    for t in range(TC):
                        mm = nc.tensor.matmul(ps[:, bank(j), P * t:P * (t + 1)], xnT[j][:, t, :], wf[:, :],
                                              start=False, stop=(t == TC - 1))
                    mm.then_inc(done, 1)
                return work

            def project(b, q, first=False):
                if q % QPH == 0:
                    if q == 0:
                        pe.wait_ge(b_h, (b + 1) * 16)
                    if not first:
                        pe.wait_ge(b_o, b * NQ + q - QPH + COPY_CREDIT)
                k_bank, q_bank = KQ_BANKS[q % QPH]
                nc.tensor.matmul(ps[:, k_bank, :], wk_s[:, q, :], hT[:, :], start=True, stop=True).then_inc(b_kps, 1)
                nc.tensor.matmul(ps[:, q_bank, :], wq_s[:, q, :], hT[:, :], start=True, stop=True).then_inc(b_qps, 1)

            def values(half):
                for t in range(TC):
                    mm = nc.tensor.matmul(ps[:, V_BANK, VH * t:VH * (t + 1)], hT[:, P * t:P * (t + 1)],
                                          wvT[:, VH * half:VH * (half + 1)], start=True, stop=True)
                mm.then_inc(b_vps, 1)

            def first_projections(row, turn, j):
                if isinstance(row, int) and row == B - 1:
                    pe.wait_ge(s_tables, 1)
                    project(0, 0, first=True)
                    values(0)
                    project(0, 1)

            pipelined(pe, ((2, feed_forward(A_FF, a_c1, a_ff)),
                           (2, first_projections),
                           (1, transposes(xn, A_TR, a_n1, a_t1)),
                           (1, spread_tables),
                           (4, transposes(hn, A_TR, a_n2, a_t2))))

            def angles(b, half, lo, hi):
                for s in range(lo, hi):
                    unit, f = order()[s // SETS_PER_SINE]
                    slot, g = unit // G, unit % G
                    n = b * SETS_ROW + half * SETS_HALF + s
                    if s < SETS:
                        if s == 0:
                            pe.wait_ge(b_sin, b * SETS_ROW + half * SETS_HALF + SET_CREDIT)
                            pe.wait_ge(b_v, b * HALVES + half + 1)
                    else:
                        pe.wait_ge(b_sin, n - SETS + 1 + SET_CREDIT)
                    if s == SETS - 1:
                        pe.wait_ge(b_xk, b * NQ + half * QPH + QPH)
                        pe.wait_ge(b_xq, b * NQ + half * QPH + QPH)
                    if unit % G == 0 and s % SETS_PER_SINE == 0:
                        pe.wait_ge(b_qr, (b * NQ + half * QPH + slot) * NF + f + 1)
                    if f == 0 and s % SETS_PER_SINE == 0:
                        pe.wait_ge(b_kr[slot][g], (b * HALVES + half + 1) * 16)
                    for t in range(SETS_PER_SINE):
                        block_at = (s % SETS_PER_SINE) * SETS_PER_SINE + t
                        keys = slice(P * block_at, P * (block_at + 1))
                        o = ps[:, (s % SETS) * SETS_PER_SINE + t, :]
                        nc.tensor.matmul(o, k_r[:, slot, 0, g, keys], q_r[:, slot, f, :], start=True, stop=False)
                        mm = nc.tensor.matmul(o, k_r[:, slot, 1, g, keys], q_r[:, slot, f, :], start=False, stop=True)
                    mm.then_inc(b_t, 1)

            def attend(b, q, last=False):
                bank, read = ((BK_A, b_xk), (BK_B, b_xq))[q % QPH]
                if not last:
                    pe.wait_ge(read, b * NQ + (q // QPH + 1) * QPH + 1)
                pe.wait_ge(b_sig, b * UNITS_ROW + G * (q + 1))
                for t in range(TC):
                    for g in range(G):
                        mm = nc.tensor.matmul(ps[R * g:R * (g + 1), bank, :], v_s[:, t, q * G + g, :],
                                              acc[:, (q % QPH) * G + g, L * t:L * (t + 1)],
                                              start=(t == 0), stop=(t == TC - 1))
                mm.then_inc(b_pv, 1)

            AHEAD = SETS
            pe.sem_inc(b_pv, PV_CREDIT)
            pe.wait_ge(a_th, B)
            pe.wait_ge(a_c2, B)
            angles(0, 0, 0, AHEAD)

            def row(b, last):
                for half in range(HALVES):
                    end = last and half == 1
                    nb, nh = (b, 1) if half == 0 else (b + 1, 0)
                    q0 = QPH * half
                    angles(b, half, AHEAD, SETS_HALF)
                    if not end:
                        project(nb, QPH * nh)
                        pe.wait_ge(b_sin, b * SETS_ROW + (half + 1) * SETS_HALF + SET_CREDIT)
                        values(nh)
                        pe.wait_ge(b_sig, b * UNITS_ROW + half * UNITS + G // 2)
                        project(nb, QPH * nh + 1)
                    attend(b, q0, end)
                    if not end:
                        angles(nb, nh, 0, AHEAD)
                    attend(b, q0 + 1, end)
            with pe.Fori(0, B - 1) as b:
                row(b, False)
            row(B - 1, True)

            def output_projection(row, turn, j):
                pe.wait_ge(c_on, row + 1)
                fill_bias(C_Y(j), 0)
                for t in range(TC):
                    mm = nc.tensor.matmul(ps[:, C_Y(j), P * t:P * (t + 1)], xin[j][:, t, :], woT[:, :],
                                          start=False, stop=(t == TC - 1))
                mm.then_inc(c_y, 1)

            pipelined(pe, ((5, feed_forward(C_FF, c_c, c_ff)), (1, output_projection),
                           (4, transposes(xn, C_TR, c_n, c_t))))

        @block.gpsimd
        def _(pool):
            nc.gpsimd.memset(ones[:, :], 1.0).then_inc(s_ones, 1)
            nc.gpsimd.memset(mhalf[:, :], -0.5).then_inc(s_ones, 1)
            nc.gpsimd.memset(v_s[:, :, :, HD:], 0.0).then_inc(s_ones, 1)
            nc.gpsimd.memset(k_r[:, :, :, :, :].bitcast(F32), 0.0).then_inc(s_ones, 1)
            pool.wait_ge(s_ones, 4)
            nc.gpsimd.memset(v_s[:, :, :, HD:HD + 1], 1.0).then_inc(s_ones, 1)

            def rsqrt(k):
                def work(row, turn, j):
                    pool.wait_ge(m_var[k], row + 1)
                    nc.gpsimd.tensor_tensor(rstd[:, j, k % 2, :], vare[:, j, k % 2, :], mhalf[:, :], ALU.pow).then_inc(m_rstd[k], 1)
                    pool.wait_ge(m_rstd[k], row + 1)
                    nc.gpsimd.tensor_tensor(nmr[:, j, k % 2, :], nmean[:, j, k % 2, :], rstd[:, j, k % 2, :], ALU.mult).then_inc(m_nmr[k], 1)
                return work

            pipelined(pool, ((3, rsqrt(1)), (0, rsqrt(0))))

            def add_beta(row, turn, j):
                pool.wait_ge(c_lx[j], (turn + 1) * 16)
                nc.gpsimd.tensor_tensor(hn[j], x1t[j], gb_bc[:, 1:2, :].to_broadcast([P, TC, D]), ALU.add).then_inc(c_xb, 1)

            pipelined(pool, ((2, add_beta), (2, rsqrt(2)), (3, rsqrt(3))))

        @block.scalar
        def _(act):
            act.wait_ge(s_wps, 1)
            act.activation(wvT[:, :], ps[:, 0, 0:P], ACT.Copy).then_inc(s_wsb, 1)
            act.activation(woT[:, :], ps[:, 0, P:2 * P], ACT.Copy).then_inc(s_wsb, 1)
            act.activation(w1T[:, :], ps[:, 0, 2 * P:3 * P], ACT.Copy).then_inc(s_wsb, 1)
            act.wait_ge(s_wps, 3)
            act.activation(w12T[:, :], ps[:, 7, 0:P], ACT.Copy).then_inc(s_wsb, 1)
            act.wait_ge(s_wps, 4)
            act.activation(wf[:, :], ps[:, 7, P:2 * P], ACT.Copy).then_inc(s_wsb, 1)
            act.wait_ge(s_setup, 1)

            def normalise(dst, src, k, done):
                def work(row, turn, j):
                    act.wait_ge(m_nmr[k], row + 1)
                    for t in range(TC):
                        last = act.activation(dst[j][:, t, :], src(j)[:, t, :], ACT.Identity,
                                              bias=nmr[:, j, k % 2, t:t + 1], scale=rstd[:, j, k % 2, t:t + 1])
                    last.then_inc(done, 1)
                return work

            def copy_transposed(dst, bank, ready, done, stored=None):
                def work(row, turn, j):
                    if stored:
                        act.wait_ge(stored[j], turn * 16 + DMA_CREDIT)
                    act.wait_ge(ready, row + 1)
                    act.activation(dst[j], by_token(bank(j)), ACT.Copy).then_inc(done, 1)
                return work

            def tanh(bank, ready, done, stored=None):
                def work(row, turn, j):
                    if stored:
                        act.wait_ge(stored[j], turn * 16 + DMA_CREDIT)
                    act.wait_ge(ready, row + 1)
                    act.activation(th[j], by_token(bank(j)), ACT.Tanh).then_inc(done, 1)
                return work

            pipelined(act, ((1, normalise(xn, lambda j: xin[j], 0, a_n1)),
                            (4, normalise(hn, lambda j: x1t[j], 1, a_n2)),
                            (2, tanh(A_FF, a_ff, a_th)),
                            (1, copy_transposed(xnT, A_TR, a_t1, a_c1)),
                            (4, copy_transposed(hTo, A_TR, a_t2, a_c2, a_sth))))

            act.sem_inc(b_sin, SET_CREDIT)

            def sines(b, half):
                for s in range(SETS_HALF):
                    m = s // SETS_PER_SINE
                    n = b * SETS_ROW + half * SETS_HALF + s
                    if s % SETS_PER_SINE == 0:
                        before = freed(m - SINS) if m >= SINS else freed(m - SINS + SINES_HALF) - ADDS_HALF
                        act.wait_ge(b_fma, b * ADDS_ROW + half * ADDS_HALF + before + SINE_CREDIT)
                    act.wait_ge(b_t, n + 1)
                    at = (s % SETS_PER_SINE) * SETS_PER_SINE * L
                    act.activation(sins[:, m % SINS, at:at + SETS_PER_SINE * L].rearrange("p (t l) -> p t l", l=L),
                                   ps[:, (s % SETS) * SETS_PER_SINE:(s % SETS + 1) * SETS_PER_SINE, :],
                                   ACT.Sin, scale=-TWO_PI_DOWN).then_inc(b_sin, 1)

            def sigmoids(b, half):
                for u in range(UNITS):
                    h = half * UNITS + u
                    act.wait_ge(b_fma, b * ADDS_ROW + half * ADDS_HALF + last_addition(u) + SINE_CREDIT)
                    act.activation(acc[:, u, :], acc[:, u, :], ACT.Sigmoid,
                                   scale=alpha_s[:, h, NF - 1:NF]).then_inc(b_sig, 1)

            def row(b, last):
                for half in range(HALVES):
                    sines(b, half)
                    sigmoids(b, half)
            with act.Fori(0, B - 1) as b:
                row(b, False)
            row(B - 1, True)

            pipelined(act, ((3, normalise(hTo, lambda j: by_token(C_Y(j)), 2, c_yn)),
                            (4, normalise(xn, lambda j: yv[j], 3, c_n)),
                            (5, tanh(C_FF, c_ff, c_th, c_st)),
                            (4, copy_transposed(xnT, C_TR, c_t, c_c))))

        @block.vector
        def _(dve):
            dve.wait_ge(s_w, N_WEIGHTS * 16)
            steps = [0]

            def then_wait(ins):
                steps[0] += 1
                ins.then_inc(s_tab_step, 1)
                dve.wait_ge(s_tab_step, steps[0])

            dve.wait_ge(s_ones, 1)
            nc.vector.tensor_copy(ones_r[:, :], ones[0:2, :])
            then_wait(nc.vector.tensor_scalar(bias_hi[:, :, :], bias2[:, :, :], cst[0:2, C_BG:C_BG + 1], None, ALU.mult))
            then_wait(nc.vector.scalar_tensor_tensor(out=bias_r[:, :, :], in0=bias2[:, :, :], scalar=cst[0:2, C_BB:C_BB + 1],
                                                     in1=bias_hi[:, :, :].bitcast(F32), op0=ALU.mult, op1=ALU.subtract))
            dve.wait_ge(s_wps, 2)
            nc.vector.tensor_copy(wq_s[:, :, :], ps[:, 1:1 + NQ, 0:P])
            nc.vector.tensor_copy(wk_s[:, :, :], ps[:, 1:1 + NQ, P:2 * P]).then_inc(s_setup, 1)

            def make_tables(row, turn, j):
                if not (isinstance(row, int) and row == 1):
                    return
                dve.wait_ge(s_const, N_CONST * 16)
                nc.vector.tensor_scalar(phit[:, :, :], phi4[:, :, :], float(1 / (2 * np.pi)), None, ALU.mult).then_inc(s_phi, 1)
                dve.wait_ge(s_wps, 5)
                nc.vector.tensor_copy(gb_bc[:, :, :], ps[:, 5, P:3 * P].rearrange("p (a n) -> p a n", a=2))
                nc.vector.tensor_copy(bv_bc[:, :], ps[:, 5, 3 * P:4 * P])
                then_wait(nc.vector.tensor_copy(alpha_bc[:, :], ps[:, 5, 0:H * NF + 1]))
                al = alpha_bc[:, 0:H * NF].rearrange("p (h f) -> p h f", h=H)
                then_wait(nc.vector.tensor_scalar(a_neg[:, :, :], al, 0.0, None, ALU.is_lt))
                then_wait(nc.vector.tensor_scalar(a_neg[:, :, :], a_neg[:, :, :], -2.0, 1.0, ALU.mult, ALU.add))
                then_wait(nc.vector.tensor_tensor(a_abs[:, :, :], al, a_neg[:, :, :], ALU.mult))
                then_wait(nc.vector.tensor_scalar(a_abs[:, :, :], a_abs[:, :, :], TINY, None, ALU.max))
                then_wait(nc.vector.tensor_tensor(alpha_s[:, :, :], a_abs[:, :, :], a_neg[:, :, :], ALU.mult))
                then_wait(nc.vector.reciprocal(a_neg[:, :, :], alpha_s[:, :, :]))
                then_wait(nc.vector.tensor_tensor(ratio[:, :, :], alpha_s[:, :, 0:NF - 1], a_neg[:, :, 1:NF], ALU.mult))
                temp = alpha_bc[:, H * NF:]
                then_wait(nc.vector.scalar_tensor_tensor(out=itemp[:, 0:1], in0=temp, scalar=-1.0, in1=temp,
                                                         op0=ALU.mult, op1=ALU.max))
                then_wait(nc.vector.tensor_scalar(itemp[:, 1:2], itemp[:, 0:1], 0.1, None, ALU.add))
                then_wait(nc.vector.reciprocal(itemp[:, 2:3], itemp[:, 1:2]))
                for f, freq in enumerate(FREQS):
                    last = nc.vector.tensor_scalar(s_f[:, f:f + 1], itemp[:, 2:3], float(1 / (np.sqrt(HD) * freq)), None, ALU.mult)
                then_wait(last)
                then_wait(nc.vector.tensor_scalar(s_f[:, :], s_f[:, :], cst[:, C_QROW:C_QROW + 1], cst[:, C_MROW:C_MROW + 1],
                                                  ALU.mult, ALU.add))
                dve.wait_ge(s_wps, 6)
                nc.vector.tensor_scalar(bq_c[:, :], ps[:, 6, 0:NQ], cst[:, C_ONE:C_ONE + 1], None, ALU.add)
                nc.vector.tensor_scalar(bk_c[:, :], ps[:, 6, NQ:2 * NQ], cst[:, C_ONE:C_ONE + 1], None, ALU.add)
                for q in range(NQ):
                    last = nc.vector.tensor_tensor(s_tab[:, q, :], ps[:, 6, P + NF * q:P + NF * (q + 1)], s_f[:, :], ALU.add)
                then_wait(last)
                nc.vector.tensor_scalar(gs[:, :, :], s_tab[:, :, :], cst[:, C_QG:C_QG + 1], None, ALU.mult)
                then_wait(nc.vector.tensor_scalar(bs[:, :, :], s_tab[:, :, :], cst[:, C_QB:C_QB + 1], None, ALU.mult))
                dve.wait_ge(s_ones, 5)
                nc.vector.tensor_copy(itemp[:, 0:1], itemp[:, 1:2]).then_inc(s_tables, 1)

            def token_stats(src, k):
                def work(row, turn, j):
                    for t in range(TC):
                        last = nc.vector.bn_stats(out=stats[:, j, k % 2, t, :], in_=src(j)[:, t, :])
                    last.then_inc(m_stats[k], 1)
                return work

            def token_moments(k):
                def work(row, turn, j):
                    dve.wait_ge(m_stats[k], row + 1)
                    alone(dve, "vector")
                    for t in range(TC):
                        last = nc.vector.bn_aggr(out=mv[:, j, k % 2, t, :], in_=stats[:, j, k % 2, t, :])
                    last.then_inc(m_mv[k], 1)
                return work

            def guard_variance(k):
                def work(row, turn, j):
                    dve.wait_ge(m_mv[k], row + 1)
                    nc.vector.tensor_scalar(nmean[:, j, k % 2, :], mv[:, j, k % 2, :, 0], -1.0, None, ALU.mult)
                    nc.vector.tensor_scalar(vare[:, j, k % 2, :], mv[:, j, k % 2, :, 1], EPS, None, ALU.add).then_inc(m_var[k], 1)
                return work

            def x_stats(row, turn, j):
                dve.wait_ge(a_x[j], (turn + 1) * 16)
                token_stats(lambda j: xin[j], 0)(row, turn, j)

            def make_x1(row, turn, j):
                dve.wait_ge(a_stx[j], turn * 16 + DMA_CREDIT)
                dve.wait_ge(a_th, row + 1)
                nc.vector.scalar_tensor_tensor(out=x1t[j], in0=th[j], scalar=0.5, in1=xin[j],
                                               op0=ALU.mult, op1=ALU.add).then_inc(a_x1, 1)

            def x1_stats(row, turn, j):
                dve.wait_ge(a_x1, row + 1 + ROW_CREDIT)
                token_stats(lambda j: x1t[j], 1)(row, turn, j)

            pipelined(dve, ((3, make_x1), (0, x_stats), (3, x1_stats), (0, token_moments(0)), (3, token_moments(1)),
                            (0, guard_variance(0)), (3, guard_variance(1)), (0, make_tables)))

            dve.sem_inc(b_fma, SINE_CREDIT)
            STEPS_QUAD = 1 + NF

            def take(b, q):
                n = b * NQ + q
                k_bank, q_bank = KQ_BANKS[q % QPH]
                dve.wait_ge(b_kps, n + 1)
                nc.vector.tensor_scalar(xk[:, :], ps[:, k_bank, :], bk_c[:, q:q + 1], None, ALU.add).then_inc(b_xk, 1)
                dve.wait_ge(b_qps, n + 1)
                nc.vector.tensor_scalar(xq[:, q % QPH, :], ps[:, q_bank, :], bq_c[:, q:q + 1], None, ALU.add).then_inc(b_xq, 1)

            def split(b, q, between=None):
                n = b * NQ + q
                first = isinstance(n, int) and n == 0
                slot = q % QPH
                k_pos, k_neg = ks[:, slot, 0, :], ks[:, slot, 1, :]

                def high(f):
                    nc.vector.tensor_scalar(hi_r[:, (f + 1) % 3, :], xq[:, slot, :], gs[:, q, f:f + 1], None, ALU.mult).then_inc(b_step, 1)

                dve.wait_ge(b_xk, n + 1)
                if not first:
                    dve.wait_ge(b_qr, n * NF - 1)
                nc.vector.tensor_scalar(hi_r[:, 0, :], xk[:, :], cst[:, C_KG:C_KG + 1], None, ALU.mult).then_inc(b_step, 1)
                dve.wait_ge(b_xq, n + 1)
                high(0)
                dve.wait_ge(b_step, n * STEPS_QUAD + 1)
                nc.vector.scalar_tensor_tensor(out=k_pos, in0=xk[:, :], scalar=cst[:, C_KB:C_KB + 1],
                                               in1=hi_r[:, 0, :].bitcast(F32), op0=ALU.mult, op1=ALU.subtract).then_inc(b_kp, 1)
                dve.wait_ge(b_kp, n + 1)
                nc.vector.tensor_scalar(k_neg, k_pos.bitcast(F32), cst[:, C_KNEG:C_KNEG + 1], None, ALU.mult).then_inc(b_ks, 1)
                if not first:
                    dve.wait_ge(b_qr, n * NF)
                high(1)
                for f in range(NF):
                    if between and f == 1:
                        between()
                    dve.wait_ge(b_step, n * STEPS_QUAD + f + 2)
                    nc.vector.scalar_tensor_tensor(out=q_r[:, slot, f, :], in0=xq[:, slot, :], scalar=bs[:, q, f:f + 1],
                                                   in1=hi_r[:, (f + 1) % 3, :].bitcast(F32),
                                                   op0=ALU.mult, op1=ALU.subtract).then_inc(b_qr, 1)
                    if f + 2 < NF:
                        if f > 0:
                            dve.wait_ge(b_qr, n * NF + f)
                        high(f + 2)

            def prepare(b, half):
                q = QPH * half
                copy_values(b, half)
                take(b, q)
                split(b, q, between=lambda: take(b, q + 1))
                split(b, q + 1)

            def copy_values(b, half):
                heads = slice(UNITS * half, UNITS * (half + 1))
                dve.wait_ge(b_vps, b * HALVES + half + 1)
                nc.vector.tensor_tensor(v_s[:, :, heads, 0:HD], ps[:, V_BANK, 0:TC * VH].rearrange("p (t h d) -> p t h d", t=TC, d=HD),
                                        bv_bc[:, VH * half:VH * (half + 1)].rearrange("p (o h d) -> p o h d", o=1, d=HD)
                                        .to_broadcast([P, TC, UNITS, HD]), ALU.add).then_inc(b_v, 1)

            def add_sines(b, half):
                base = b * ADDS_ROW + half * ADDS_HALF + SINE_CREDIT
                for m, (unit, f) in enumerate(order()):
                    q = half * QPH + unit // G
                    h = q * G + unit % G
                    dve.wait_ge(b_sin, b * SETS_ROW + half * SETS_HALF + SETS_PER_SINE * (m + 1) + SET_CREDIT)
                    if f == 0:
                        continue
                    if f == 1:
                        dve.wait_ge(b_pv, b * NQ + q - QPH + 1 + PV_CREDIT)
                        before = sins[:, (m - 2) % SINS, :]
                    else:
                        dve.wait_ge(b_fma, base + added(m) - 2)
                        before = acc[:, unit, :]
                    ins = nc.vector.scalar_tensor_tensor(out=acc[:, unit, :], in0=before, scalar=ratio[:, h, f - 1:f],
                                                         in1=sins[:, m % SINS, :], op0=ALU.mult, op1=ALU.add)
                    ins.then_inc(b_fma, 1)

            def copy_pv(b, half, q):
                slot = q % QPH
                dve.wait_ge(b_st[slot], (b * HALVES + half) * STORES * 16 + STORE_CREDIT)
                dve.wait_ge(b_pv, b * NQ + q + 1 + PV_CREDIT)
                nc.vector.tensor_copy(o_sb[:, slot, :], ps[:, (BK_A, BK_B)[slot], :]).then_inc(b_o, 1)

            def invert_denominators(i):
                dve.wait_ge(b_den, (i + 1) * 16)
                nc.vector.tensor_scalar(den_row[:, :], den_row[:, :], 1e-10, None, ALU.add).then_inc(b_eps, 1)
                dve.wait_ge(b_eps, i + 1)
                nc.vector.reciprocal(den_row[:, :], den_row[:, :]).then_inc(b_rden, 1)

            dve.sem_inc(b_o, COPY_CREDIT)
            prepare(0, 0)
            for j in range(NS):
                dve.wait_ge(a_stx[j], B // NS * 16 + DMA_CREDIT)
                dve.wait_ge(a_sth[j], B // NS * 16 + DMA_CREDIT)

            def row(b, last):
                for half in range(HALVES):
                    end = half == 1 and last
                    add_sines(b, half)
                    nb, nh = (b, 1) if half == 0 else (b + 1, 0)
                    if not end:
                        prepare(nb, nh)
                    for q in range(QPH * half, QPH * (half + 1)):
                        copy_pv(b, half, q)
                    if half == 0:
                        invert_denominators(b)
            with dve.Fori(0, B - 1) as b:
                row(b, False)
            row(B - 1, True)
            invert_denominators(B)

            def normalise_heads(row, turn, j):
                dve.wait_ge(c_lo[j], (turn + 1) * 32)
                nc.vector.tensor_tensor(xin[j], xin[j], rdc[j].rearrange("p (t d) -> p t d", t=TC), ALU.mult).then_inc(c_on, 1)

            def times_gamma(row, turn, j):
                dve.wait_ge(c_yn, row + 1)
                nc.vector.tensor_tensor(hTo[j], hTo[j], gb_bc[:, 0:1, :].to_broadcast([P, TC, D]), ALU.mult).then_inc(c_yg, 1)

            def add_attention(row, turn, j):
                dve.wait_ge(c_xb, row + 1 + ROW_CREDIT)
                dve.wait_ge(c_yg, row + 1)
                nc.vector.tensor_tensor(yv[j], hTo[j], hn[j], ALU.add).then_inc(c_x2, 1)

            def make_out(row, turn, j):
                dve.wait_ge(c_th, row + 1)
                nc.vector.scalar_tensor_tensor(out=th[j], in0=th[j], scalar=0.5, in1=yv[j],
                                               op0=ALU.mult, op1=ALU.add).then_inc(c_out, 1)

            def y_stats(row, turn, j):
                dve.wait_ge(c_y, row + 1 + ROW_CREDIT)
                token_stats(lambda j: by_token(C_Y(j)), 2)(row, turn, j)

            def x2_stats(row, turn, j):
                dve.wait_ge(c_x2, row + 1)
                token_stats(lambda j: yv[j], 3)(row, turn, j)

            pipelined(dve, ((1, normalise_heads), (6, make_out), (2, y_stats), (3, times_gamma), (2, token_moments(2)),
                            (3, add_attention), (2, guard_variance(2)), (3, x2_stats), (3, token_moments(3)),
                            (3, guard_variance(3))))


NAMES = ['L0_attn_x', 'L0_attn_Wq', 'L0_attn_bq', 'L0_attn_Wk', 'L0_attn_bk', 'L0_attn_Wv', 'L0_attn_bv',
         'L0_attn_Wo', 'L0_attn_bo', 'L0_attn_alpha', 'L0_attn_phi', 'L0_attn_temperature', 'L0_attn_gamma',
         'L0_attn_beta', 'L0_ffn_weight', 'L0_ffn_aux_weight1', 'L0_ffn_aux_weight2', 'L0_ffn_bias']


def kernel(**inputs):
    import concourse.bacc as bacc
    from concourse.bass_utils import run_bass_kernel_spmd

    nc = bacc.Bacc("TRN2", target_bir_lowering=False, num_devices=1)
    arrays, args = {}, []
    for name in NAMES:
        a = np.ascontiguousarray(inputs[name])
        arrays[f"in_{name}"] = a
        args.append(nc.dram_tensor(f"in_{name}", a.shape, mybir.dt.from_np(a.dtype), kind="ExternalInput").ap())
    c = constants()
    arrays["in_consts"] = c
    args.append(nc.dram_tensor("in_consts", c.shape, mybir.dt.float32, kind="ExternalInput").ap())
    args.append(nc.dram_tensor("out", (B, L, D), mybir.dt.float32, kind="ExternalOutput").ap())
    build(nc, *args)
    r = run_bass_kernel_spmd(nc, [arrays], core_ids=[0])
    return r.results[0]["out"]
```
